# Optimizing a Trainium2 kernel written in Bass

```python
import numpy as np
import jax
import jax.numpy as jnp

def _softmax(x, axis=-1):
    return jax.nn.softmax(x, axis=axis)

def _gelu(x):
    return jax.nn.gelu(x, approximate=True)

def _silu(x):
    return jax.nn.silu(x)

def _sigmoid(x):
    return jax.nn.sigmoid(x)

def _layernorm(x, axis=-1, eps=1e-05):
    m = jnp.mean(x, axis=axis, keepdims=True)
    v = jnp.var(x, axis=axis, keepdims=True)
    return (x - m) / jnp.sqrt(v + eps)

def _scatter_add(tgt, idx, src, axis=0):
    return tgt.at[idx].add(src)

def _segment_sum(src, seg, n):
    return jax.ops.segment_sum(src, seg, n)
kernel_name = 'mk_xattn_seq_d2_seqx_r2_6231ba'

def setup_inputs(seed: int=0):
    np.random.seed(seed)
    _w = jnp.asarray

    def _rec_inputs():
        import jax
        import jax.numpy as jnp
        _rk = jax.random.key(seed)
        x = 7.22e-05 + 1 * jax.random.normal(jax.random.fold_in(_rk, 1), (2, 2048, 512), jnp.float32)
        _lenS = 2048 - jax.random.randint(jax.random.fold_in(_rk, 7), (2,), 0, max(1, 2048 // 4) + 1, jnp.int32)
        _lenS2 = 128 - jax.random.randint(jax.random.fold_in(_rk, 8), (2,), 0, max(1, 128 // 4) + 1, jnp.int32)
        _ctx_1024P = jax.random.normal(jax.random.fold_in(_rk, 11), (2, 16, 512), jnp.float32)
        _ctx_1024c = jax.random.dirichlet(jax.random.fold_in(_rk, 511), 0.3 * jnp.ones((16,), jnp.float32), (2, 128))
        _ctx_1024t = jnp.einsum('bsk,bkd->bsd', _ctx_1024c, _ctx_1024P)
        _ctx_1024t = _ctx_1024t * jax.lax.rsqrt(jnp.mean(jnp.square(_ctx_1024t)) + 1e-12) * 0.953939
        ctx_1024 = 4.13588e-05 + 0.999923 * (_ctx_1024t + 0.3 * jax.random.normal(jax.random.fold_in(_rk, 611), (2, 128, 512), jnp.float32))
        _validS = jnp.arange(2048)[None, :] < _lenS[:, None]
        _validS2 = jnp.arange(128)[None, :] < _lenS2[:, None]
        _causal = jnp.tril(jnp.ones((2048, 2048), dtype=bool))
        mask_BxSxS2_ik1 = jnp.where(jnp.broadcast_to(_validS2[:, None, :], (2, 2048, 128)), 1, 0).astype(jnp.int32)
        return (x, ctx_1024, mask_BxSxS2_ik1)
    x, ctx_1024, mask_BxSxS2_ik1 = _rec_inputs()

    def _L0_xattn_setup():
        import jax, jax.numpy as jnp
        import numpy as np
        B, T, D, H, DK = (4, 1024, 512, 16, 64)
        key = jax.random.key(seed)
        ks = jax.random.split(key, 9)
        s = 0.02
        return {'q': jax.random.normal(ks[0], (B, T, D), jnp.float32), 'k': jax.random.normal(ks[1], (B, T, D), jnp.float32), 'v': jax.random.normal(ks[2], (B, T, D), jnp.float32), 'attn_mask': jax.random.randint(ks[3], (B, T, T), 0, 2, jnp.int32), 'Wq': jax.random.normal(ks[4], (D, H * DK), jnp.float32) * s, 'bq': jnp.zeros((H * DK,), jnp.float32), 'Wk': jax.random.normal(ks[5], (D, H * DK), jnp.float32) * s, 'bk': jnp.zeros((H * DK,), jnp.float32), 'Wv': jax.random.normal(ks[6], (D, H * DK), jnp.float32) * s, 'bv': jnp.zeros((H * DK,), jnp.float32), 'Wo': jax.random.normal(ks[7], (H * DK, D), jnp.float32) * s, 'bo': jnp.zeros((D,), jnp.float32), 'gamma': jnp.ones((D,), jnp.float32), 'beta': jnp.zeros((D,), jnp.float32)}
    _L0_xattn_all = _L0_xattn_setup()
    _L0_xattn_in = {k: v for k, v in _L0_xattn_all.items() if k in ('Wq', 'bq', 'Wk', 'bk', 'Wv', 'bv', 'Wo', 'bo', 'gamma', 'beta')}
    del _L0_xattn_all

    def _L1_xattn_setup():
        import jax, jax.numpy as jnp
        import numpy as np
        B, S, H = (2, 1024, 512)
        NH = 16
        HD = H // NH
        LN_EPS = 1e-05

        def _split_heads(x):
            b, s, _ = x.shape
            return x.reshape(b, s, NH, HD).transpose(0, 2, 1, 3)
        key = jax.random.key(seed)
        ks = jax.random.split(key, 10)
        sc = 1.0 / np.sqrt(H)
        return {'query': jax.random.normal(ks[0], (B, S, H), jnp.float32), 'key': jax.random.normal(ks[1], (B, S, H), jnp.float32), 'value': jax.random.normal(ks[2], (B, S, H), jnp.float32), 'Wq': jax.random.normal(ks[3], (H, H), jnp.float32) * sc, 'Wk': jax.random.normal(ks[4], (H, H), jnp.float32) * sc, 'Wv': jax.random.normal(ks[5], (H, H), jnp.float32) * sc, 'Wo': jax.random.normal(ks[6], (H, H), jnp.float32) * sc, 'bo': jnp.zeros((H,), jnp.float32), 'ln_gamma': jnp.ones((H,), jnp.float32), 'ln_beta': jnp.zeros((H,), jnp.float32)}
    _L1_xattn_all = _L1_xattn_setup()
    _L1_xattn_in = {k: v for k, v in _L1_xattn_all.items() if k in ('Wq', 'Wk', 'Wv', 'Wo', 'bo', 'ln_gamma', 'ln_beta')}
    del _L1_xattn_all
    return {'x': x, 'ctx_1024': ctx_1024, 'mask_BxSxS2_ik1': mask_BxSxS2_ik1, 'L0_xattn_Wq': _L0_xattn_in['Wq'], 'L0_xattn_bq': _L0_xattn_in['bq'], 'L0_xattn_Wk': _L0_xattn_in['Wk'], 'L0_xattn_bk': _L0_xattn_in['bk'], 'L0_xattn_Wv': _L0_xattn_in['Wv'], 'L0_xattn_bv': _L0_xattn_in['bv'], 'L0_xattn_Wo': _L0_xattn_in['Wo'], 'L0_xattn_bo': _L0_xattn_in['bo'], 'L0_xattn_gamma': _L0_xattn_in['gamma'], 'L0_xattn_beta': _L0_xattn_in['beta'], 'L1_xattn_Wq': _L1_xattn_in['Wq'], 'L1_xattn_Wk': _L1_xattn_in['Wk'], 'L1_xattn_Wv': _L1_xattn_in['Wv'], 'L1_xattn_Wo': _L1_xattn_in['Wo'], 'L1_xattn_bo': _L1_xattn_in['bo'], 'L1_xattn_ln_gamma': _L1_xattn_in['ln_gamma'], 'L1_xattn_ln_beta': _L1_xattn_in['ln_beta']}

def reference(x, ctx_1024, mask_BxSxS2_ik1, L0_xattn_Wq, L0_xattn_bq, L0_xattn_Wk, L0_xattn_bk, L0_xattn_Wv, L0_xattn_bv, L0_xattn_Wo, L0_xattn_bo, L0_xattn_gamma, L0_xattn_beta, L1_xattn_Wq, L1_xattn_Wk, L1_xattn_Wv, L1_xattn_Wo, L1_xattn_bo, L1_xattn_ln_gamma, L1_xattn_ln_beta):
    import jax
    import jax.numpy as jnp

    def _L0_xattn_ref(q, k, v, attn_mask, Wq, bq, Wk, bk, Wv, bv, Wo, bo, gamma, beta):
        import jax, jax.numpy as jnp
        import numpy as np
        B, T, D, H, DK = (4, 1024, 512, 16, 64)
        Bn, Tq, _ = q.shape
        Tk = k.shape[1]
        residual = q
        mask = attn_mask.astype(jnp.float32)
        qh = (q @ Wq + bq).reshape(Bn, Tq, H, DK)
        kh = (k @ Wk + bk).reshape(Bn, Tk, H, DK)
        vh = (v @ Wv + bv).reshape(Bn, Tk, H, DK)
        attn = jnp.einsum('bqhd,bkhd->hbqk', qh, kh)
        attn = attn * mask[None]
        attn = attn - jnp.max(attn)
        attn = jnp.exp(attn) * mask[None]
        attn = attn / (jnp.sum(attn, axis=-1, keepdims=True) + 1e-15)
        out = jnp.einsum('hbqk,bkhd->bqhd', attn, vh).reshape(Bn, Tq, H * DK)
        out = out @ Wo + bo
        x = out + residual
        mu = jnp.mean(x, axis=-1, keepdims=True)
        var = jnp.mean((x - mu) ** 2, axis=-1, keepdims=True)
        return (x - mu) / jnp.sqrt(var + 1e-05) * gamma + beta

    def _L1_xattn_ref(query, key, value, Wq, Wk, Wv, Wo, bo, ln_gamma, ln_beta):
        import jax, jax.numpy as jnp
        import numpy as np
        B, S, H = (2, 1024, 512)
        NH = 16
        HD = H // NH
        LN_EPS = 1e-05

        def _split_heads(x):
            b, s, _ = x.shape
            return x.reshape(b, s, NH, HD).transpose(0, 2, 1, 3)
        q = _split_heads(query @ Wq.T)
        k = _split_heads(key @ Wk.T)
        v = _split_heads(value @ Wv.T)
        scaling = 1.0 / jnp.sqrt(jnp.asarray(HD, q.dtype))
        logits = scaling * jnp.einsum('bhqd,bhkd->bhqk', q, k)
        attn = jax.nn.softmax(logits, axis=-1)
        ctx = jnp.einsum('bhqk,bhkd->bhqd', attn, v)
        ctx = ctx.transpose(0, 2, 1, 3).reshape(query.shape[0], q.shape[2], H)
        projected = ctx @ Wo.T + bo
        resid = query + projected
        mu = jnp.mean(resid, axis=-1, keepdims=True)
        var = jnp.var(resid, axis=-1, keepdims=True)
        return (resid - mu) / jnp.sqrt(var + LN_EPS) * ln_gamma + ln_beta
    x = _L0_xattn_ref(x, ctx_1024, ctx_1024, mask_BxSxS2_ik1, L0_xattn_Wq, L0_xattn_bq, L0_xattn_Wk, L0_xattn_bk, L0_xattn_Wv, L0_xattn_bv, L0_xattn_Wo, L0_xattn_bo, L0_xattn_gamma, L0_xattn_beta)
    x = _L1_xattn_ref(x, ctx_1024, ctx_1024, L1_xattn_Wq, L1_xattn_Wk, L1_xattn_Wv, L1_xattn_Wo, L1_xattn_bo, L1_xattn_ln_gamma, L1_xattn_ln_beta)
    return x

_drawn_inputs = setup_inputs


def setup_inputs(seed=0):
    import zlib

    import numpy as np

    out = dict(_drawn_inputs(seed))
    spreads = {'L0_xattn_bq': (0.0, 0.275),
     'L0_xattn_bk': (0.0, 2.0),
     'L0_xattn_bv': (0.0, 0.1),
     'L0_xattn_bo': (0.0, 0.1),
     'L0_xattn_gamma': (1.0, 0.2),
     'L0_xattn_beta': (0.0, 0.1),
     'L1_xattn_bo': (0.0, 0.1),
     'L1_xattn_ln_gamma': (1.0, 0.2),
     'L1_xattn_ln_beta': (0.0, 0.1)}
    factors = {}
    for name, (base, spread) in spreads.items():
        noise = np.random.default_rng([zlib.crc32(name.encode()), seed]).standard_normal(out[name].shape)
        drawn = base * np.exp(spread * noise) if base else spread * noise
        out[name] = jnp.asarray(drawn.astype(out[name].dtype))
    for name, factor in factors.items():
        out[name] = (out[name] * factor).astype(out[name].dtype)
    return out
```

```python
import math
from contextlib import ExitStack

import numpy as np

import concourse.bass as bass
from concourse import mybir

P = 128
B, S, D, KEYS = 2, 2048, 512, 128
H0, DK0 = 16, 64
H1, DK1 = 16, 32
E0, E1 = H0 * DK0, H1 * DK1
QB = 512
QH = QB // B
NB = B * S // QB
QT = QB // P
KC = D // P
C0, C1 = E0 // P, E1 // P
HC0, HC1 = P // DK0, P // DK1
G = 4
HG = H0 // G
LN_EPS = 1e-5
SUM_EPS = 1e-15
SCALE1 = 1.0 / math.sqrt(DK1)
HEADROOM = 40.0
SUMW = QB + 8


def cross_attention_program(nc, x_t, x_n, mask_t, ctx_t, wq0, wk0, wv0, wo0, wq1, wk1, wv1, wo1,
                            bq0, bk0, bv0, bo0, gamma0, beta0, gcol0, bcol0, bo1, gamma1, beta1,
                            sum_sel, head_sel0, head_sel1, identity, out):
    f32, f32r, i32 = mybir.dt.float32, mybir.dt.float32r, mybir.dt.int32
    ALU, ACT, AX = mybir.AluOpType, mybir.ActivationFunctionType, mybir.AxisListType
    MAX = bass.bass_isa.ReduceOp.max

    u_dram = nc.dram_tensor("u_dram", [NB, P, C0 * QB], f32, kind="Internal").ap()
    sums_dram = nc.dram_tensor("sums_dram", [NB, P, SUMW], f32, kind="Internal").ap()

    def at(dram, i):
        return dram[i] if isinstance(i, int) else dram[bass.ds(i, 1)].rearrange("a p n -> (a p) n")

    with ExitStack() as ctx:
        def sb(stack, name, shape, dt=f32):
            return stack.enter_context(nc.sbuf_tensor(name, shape, dt))

        def sem(name):
            return ctx.enter_context(nc.semaphore(name))

        k1_hi, k1_lo = (sb(ctx, n, [P, C1, B * KEYS], f32r) for n in ("k1_hi", "k1_lo"))
        v1 = sb(ctx, "v1", [P, B, E1])
        summer = sb(ctx, "summer", [P, HG, 32])
        run_max = sb(ctx, "run_max", [P, 1])
        with ExitStack() as late:
            resid = sb(late, "resid", [P, QT, D])
            z1 = sb(late, "z1", [P, QT, D])
        w_stage = sb(ctx, "w_stage", [P, 8 * 512])
        with ExitStack() as shared:
            yt_hi, yt_lo = (sb(shared, n, [P, KC, QB], f32r) for n in ("yt_hi", "yt_lo"))
        scores = sb(ctx, "scores", [P, H0, QB])

        with ExitStack() as p1:
            k0_hi, k0_lo = (sb(p1, n, [P, C0, B * KEYS], f32r) for n in ("k0_hi", "k0_lo"))
            v0 = sb(p1, "v0", [P, B, E0])
            wq0_hi, wq0_lo = (sb(p1, n, [P, KC, E0], f32r) for n in ("wq0_hi", "wq0_lo"))
            bq_sb = sb(p1, "bq_sb", [P, C0])
            bk_sb = sb(p1, "bk_sb", [P, C0])
            maxes = sb(p1, "maxes", [P, H0])
            tile_mx = sb(p1, "tile_mx", [P, 1])
            all_mx = sb(p1, "all_mx", [P, 1])
            neg_mx = sb(p1, "neg_mx", [P, 1])
            x_raw = sb(p1, "x_raw", [P, KC, QB])
            mask_raw = sb(p1, "mask_raw", [P, QB], i32)
            mask_f = sb(p1, "mask_f", [P, QB])
            with ExitStack() as setup:
                wk0_sb = sb(setup, "wk0_sb", [P, KC, E0])
                wv0_sb = sb(setup, "wv0_sb", [P, KC, E0])
                wk1_sb = sb(setup, "wk1_sb", [P, KC, E1])
                wv1_sb = sb(setup, "wv1_sb", [P, KC, E1])
                ctx_sb = sb(setup, "ctx_sb", [P, KC, B * KEYS])
                bv_sb = sb(setup, "bv_sb", [P, E0])
            x_hi, x_lo = (sb(p1, n, [P, KC, QB], f32r) for n in ("x_hi", "x_lo"))
            q0_hi, q0_lo = (sb(p1, n, [P, C0, QB], f32r) for n in ("q0_hi", "q0_lo"))
            u_out = sb(p1, "u_out", [P, C0, QB])
            sums_out = sb(p1, "sums_out", [P, SUMW])

        with ExitStack() as p2:
            wo0_hi, wo0_lo = (sb(p2, n, [P, C0, D], f32r) for n in ("wo0_hi", "wo0_lo"))
            wq1_hi, wq1_lo = (sb(p2, n, [P, KC, E1], f32r) for n in ("wq1_hi", "wq1_lo"))
            wo1_hi, wo1_lo = (sb(p2, n, [P, C1, D], f32r) for n in ("wo1_hi", "wo1_lo"))
            hs0 = sb(p2, "hs0", [P, C0, P], f32r)
            hs1 = sb(p2, "hs1", [P, C1, P], f32r)
            ident = sb(p2, "ident", [P, P])
            u_in = sb(p2, "u_in", [P, C0, QB])
            sums_in = sb(p2, "sums_in", [P, SUMW])
            eps_f = sb(p2, "eps_f", [P, 1])
            m_eps = sb(p2, "m_eps", [P, 1])
            den = sb(p2, "den", [P, QB])
            r0_hi, r0_lo = (sb(p2, n, [P, QB], f32r) for n in ("r0_hi", "r0_lo"))
            r1_hi, r1_lo = (sb(p2, n, [P, QB], f32r) for n in ("r1_hi", "r1_lo"))
            a0_hi, a0_lo = (sb(p2, n, [P, 2, QB], f32r) for n in ("a0_hi", "a0_lo"))
            q1_hi, q1_lo = (sb(p2, n, [P, C1, QB], f32r) for n in ("q1_hi", "q1_lo"))
            u1 = sb(p2, "u1", [P, C1, QB])
            z0 = sb(p2, "z0", [P, QT, D])
            bo0_b, g0_b, bb1_b, g1_b, be1_b = (sb(p2, n, [P, D]) for n in
                                               ("bo0_b", "g0_b", "bb1_b", "g1_b", "be1_b"))
            g0_col = sb(p2, "g0_col", [P, KC])
            b0_col = sb(p2, "b0_col", [P, KC])
            bq1_sb = sb(p2, "bq1_sb", [P, C1])
            st0, st1 = (sb(p2, n, [P, QT, 6]) for n in ("st0", "st1"))
            mv0, mv1 = (sb(p2, n, [P, QT, 2]) for n in ("mv0", "mv1"))
            rs0, rs1 = (sb(p2, n, [P, QT]) for n in ("rs0", "rs1"))
            mhalf = sb(p2, "mhalf", [P, QT])
            mx1 = sb(p2, "mx1", [P, H1])
            amx1 = sb(p2, "amx1", [P, H1])
            sh1 = sb(p2, "sh1", [P, H1])
        u1_flat = u1[:].rearrange("p c n -> p (c n)")
        sel0_raw, sel1_raw = u1_flat[:, 0:C0 * P], u1_flat[:, C0 * P:(C0 + C1) * P]
        beta0_b = u1_flat[:, (C0 + C1) * P:(C0 + C1) * P + D]
        s_stage = scores[:, 0:8, :].rearrange("p h n -> p (h n)")

        bank = [ctx.enter_context(nc.psum_tensor(f"bank{n}", [P, 512], f32)) for n in range(8)]
        A_BANKS, B_BANKS, U_BANKS, SUM_BANK = bank[0:2], bank[2:5], bank[5:7], bank[7]
        Z_BANKS, R_BANKS = bank[0:4], bank[4:8]
        PV_BANKS = [R_BANKS[3], R_BANKS[0], R_BANKS[1], R_BANKS[2]]

        setup_loaded = [sem(f"setup_loaded{n}") for n in range(5)]
        small_loaded = sem("small_loaded")
        x_loaded, mask_loaded = sem("x_loaded"), sem("mask_loaded")
        u_stored, sums_stored = sem("u_stored"), sem("sums_stored")
        wo0_loaded, w1_loaded, consts_loaded = sem("wo0_loaded"), sem("w1_loaded"), sem("consts_loaded")
        u_loaded, sums_loaded, xn_loaded, out_stored = (sem(n) for n in (
            "u_loaded", "sums_loaded", "xn_loaded", "out_stored"))
        kv_psum_ready, k_hi_ready, kv_done, wq0_hi_ready, wq0_ready = (sem(n) for n in (
            "kv_psum_ready", "k_hi_ready", "kv_done", "wq0_hi_ready", "wq0_ready"))
        x_hi_ready, x_ready = sem("x_hi_ready"), sem("x_ready")
        mask_ready = sem("mask_ready")
        q_psum_ready, q_hi_ready, q_ready = sem("q_psum_ready"), sem("q_hi_ready"), sem("q_ready")
        logits_ready, masked_ready = sem("logits_ready"), sem("masked_ready")
        tile_max_ready, all_max_ready, run_max_ready, shift_ready, m_saved = (sem(n) for n in (
            "tile_max_ready", "all_max_ready", "run_max_ready", "shift_ready", "m_saved"))
        exp_ready, probs_ready = sem("exp_ready"), sem("probs_ready")
        u_psum_ready, sums_psum_ready = sem("u_psum_ready"), sem("sums_psum_ready")
        u_saved = sem("u_saved")
        m_eps_ready, mhalf_ready, wo0_hi_ready, wo0_ready, w1_hi_ready, w1_ready, hs_ready, bb1_ready = (
            sem(n) for n in ("m_eps_ready", "mhalf_ready", "wo0_hi_ready", "wo0_ready", "w1_hi_ready",
                             "w1_ready", "hs_ready", "bb1_ready"))
        bq1_psum_ready, bq1_ready = sem("bq1_psum_ready"), sem("bq1_ready")
        eps_ready, den0_ready, rec0_ready, r0_hi_ready, r0_ready = (sem(n) for n in (
            "eps_ready", "den0_ready", "rec0_ready", "r0_hi_ready", "r0_ready"))
        bc0_ready, attn0_ready, a0_hi_ready, a0_ready = (sem(n) for n in (
            "bc0_ready", "attn0_ready", "a0_hi_ready", "a0_ready"))
        a0_used = sem("a0_used")
        xb_ready, o0_ready = sem("xb_ready"), sem("o0_ready")
        z0_ready, bn0_ready, mv0_ready, n0_ready = (sem(n) for n in (
            "z0_ready", "bn0_ready", "mv0_ready", "n0_ready"))
        var0_ready, rstd0_ready, rg_ready, resid_ready = (sem(n) for n in (
            "var0_ready", "rstd0_ready", "rg_ready", "resid_ready"))
        yt_psum_ready, yt_hi_ready, yt_ready = (sem(n) for n in (
            "yt_psum_ready", "yt_hi_ready", "yt_ready"))
        q1_psum_ready, q1_hi_ready, q1_ready = (sem(n) for n in (
            "q1_psum_ready", "q1_hi_ready", "q1_ready"))
        logits1_ready, scores1_ready = sem("logits1_ready"), sem("scores1_ready")
        amax1_ready, shift1_ready = sem("amax1_ready"), sem("shift1_ready")
        probs1_ready = sem("probs1_ready")
        sums1_psum_ready, den1_ready, rec1_ready, r1_hi_ready, r1_ready = (sem(n) for n in (
            "sums1_psum_ready", "den1_ready", "rec1_ready", "r1_hi_ready", "r1_ready"))
        u1_psum_ready, u1_saved, bc1_ready, attn1_ready, a1_hi_ready, a1_ready = (sem(n) for n in (
            "u1_psum_ready", "u1_saved", "bc1_ready", "attn1_ready", "a1_hi_ready", "a1_ready"))
        o1_ready = sem("o1_ready")
        z1_ready, bn1_ready, mv1_ready, ng1_ready, out_ready = (sem(n) for n in (
            "z1_ready", "bn1_ready", "mv1_ready", "ng1_ready", "out_ready"))
        var1_ready, rstd1_ready = sem("var1_ready"), sem("rstd1_ready")

        block = ctx.enter_context(nc.Block())

        @block.sync
        def _(sp):
            for dst, src in ((ctx_sb, ctx_t),):
                sp.dma_start(dst[:], src.rearrange("(c p) n -> p c n", p=P)).then_inc(setup_loaded[0], 16)
            sp.dma_start(wk0_sb[:], wk0.rearrange("(c p) n -> p c n", p=P)).then_inc(setup_loaded[0], 16)
            for dst, src in ((bk_sb, bk0), (bq_sb, bq0), (summer, sum_sel)):
                sp.dma_start(dst[:], src).then_inc(small_loaded, 16)
            sp.dma_start(bv_sb[:], bv0.partition_broadcast(P)).then_inc(small_loaded, 16)
            for n, (dst, src) in enumerate(((wv0_sb, wv0), (wk1_sb, wk1), (wv1_sb, wv1))):
                sp.dma_start(dst[:], src.rearrange("(c p) n -> p c n", p=P)).then_inc(setup_loaded[1 + n], 16)
            sp.dma_start(w_stage[:].rearrange("p (c n) -> p c n", c=KC),
                         wq0.rearrange("(c p) n -> p c n", p=P)).then_inc(setup_loaded[4], 16)

            def load_x(i):
                if not (isinstance(i, int) and i == 0):
                    sp.wait_ge(x_ready, i)
                sp.dma_start(x_raw[:], at(x_t, i).rearrange("(c p) n -> p c n", p=P)).then_inc(x_loaded, 16)

            def load_mask(i):
                if not (isinstance(i, int) and i == 0):
                    sp.wait_ge(mask_ready, i)
                sp.dma_start(mask_raw[:], at(mask_t, i)).then_inc(mask_loaded, 16)

            load_x(0)
            load_mask(0)
            load_x(1)
            load_mask(1)
            sp.wait_ge(wq0_ready, 1)
            sp.dma_start(w_stage[:].rearrange("p (c n) -> p c n", c=C0),
                         wo0.rearrange("(c p) n -> p c n", p=P)).then_inc(wo0_loaded, 16)
            with sp.Fori(1, NB - 1) as i:
                load_x(i + 1)
                load_mask(i + 1)

            sp.wait_ge(sums_psum_ready, NB)
            sp.wait_ge(u_saved, (C0 + 1) * NB)
            sp.wait_ge(u_stored, 16 * NB)
            sp.wait_ge(sums_stored, 16 * NB)
            sp.wait_ge(m_saved, NB)

            def load_sums(i, n):
                if not (isinstance(n, int) and n == 0):
                    sp.wait_ge(den0_ready, n)
                    nc.sync.nop(nofuse=True)
                sp.dma_start(sums_in[:], at(sums_dram, i)).then_inc(sums_loaded, 16)

            load_sums(0, 0)
            sp.dma_start(u_in[:].rearrange("p c n -> p (c n)"), at(u_dram, 0)).then_inc(u_loaded, 16)
            for dst, src in ((sel0_raw, head_sel0), (sel1_raw, head_sel1)):
                sp.dma_start(dst, src).then_inc(consts_loaded, 16)
            sp.dma_start(s_stage[:, 0:2048].rearrange("p (c n) -> p c n", c=KC),
                         wq1.rearrange("(c p) n -> p c n", p=P)).then_inc(w1_loaded, 16)
            sp.dma_start(s_stage[:, 2048:4096].rearrange("p (c n) -> p c n", c=C1),
                         wo1.rearrange("(c p) n -> p c n", p=P)).then_inc(w1_loaded, 16)
            sp.dma_start(z0[:], at(x_n, 0).rearrange("(t p) n -> p t n", p=P)).then_inc(xn_loaded, 16)
            for dst, src in ((bo0_b, bo0), (g0_b, gamma0), (bb1_b, bo1), (g1_b, gamma1), (be1_b, beta1)):
                sp.dma_start(dst[:], src.partition_broadcast(P)).then_inc(consts_loaded, 16)
            sp.dma_start(beta0_b, beta0.partition_broadcast(P)).then_inc(consts_loaded, 16)
            for dst, src in ((ident, identity), (g0_col, gcol0), (b0_col, bcol0)):
                sp.dma_start(dst[:], src).then_inc(consts_loaded, 16)
            load_sums(1, 1)
            with sp.Fori(1, NB) as i:
                sp.wait_ge(a0_ready, C0 * i)
                sp.dma_start(u_in[:].rearrange("p c n -> p (c n)"), at(u_dram, i)).then_inc(u_loaded, 16)
                load_sums((i + 1) % NB, i + 1)
                sp.wait_ge(resid_ready, i)
                nc.sync.nop(nofuse=True)
                sp.wait_ge(yt_psum_ready, KC * i)
                sp.dma_start(z0[:], at(x_n, i).rearrange("(t p) n -> p t n", p=P)).then_inc(xn_loaded, 16)
            sp.wait_ge(sums_loaded, 16 * (NB + 1))
            sp.wait_ge(out_stored, 16 * NB)

        @block.tensor
        def _(pe):
            n_bank = [0]

            def setup_bank():
                n = n_bank[0]
                n_bank[0] += 1
                if n >= 8:
                    pe.wait_ge(kv_done, n - 7)
                return bank[n % 8]

            def keys(w, chunks):
                for c in range(chunks):
                    dst = setup_bank()[:, 0:B * KEYS]
                    for k in range(KC):
                        last = nc.tensor.matmul(dst, w[:, k, c * P:(c + 1) * P], ctx_sb[:, k, :],
                                                start=(k == 0), stop=(k == KC - 1))
                    last.then_inc(kv_psum_ready, 1)

            def values(w, width):
                for b in range(B):
                    for n in range(width // 512):
                        dst = setup_bank()[:]
                        for k in range(KC):
                            last = nc.tensor.matmul(dst, ctx_sb[:, k, b * KEYS:(b + 1) * KEYS],
                                                    w[:, k, n * 512:(n + 1) * 512],
                                                    start=(k == 0), stop=(k == KC - 1))
                        last.then_inc(kv_psum_ready, 1)

            pe.wait_ge(setup_loaded[0], 32)
            keys(wk0_sb, C0)
            pe.wait_ge(setup_loaded[1], 16)
            values(wv0_sb, E0)
            pe.wait_ge(setup_loaded[2], 16)
            keys(wk1_sb, C1)
            pe.wait_ge(setup_loaded[3], 16)
            values(wv1_sb, E1)
            pe.wait_ge(kv_done, n_bank[0])

            def split_product(dst, lhs, rhs, first, last):
                (lh, ll), (rh, rl) = lhs, rhs
                nc.tensor.matmul(dst, lh, rl, start=first, stop=False)
                nc.tensor.matmul(dst, ll, rh, start=False, stop=False)
                return nc.tensor.matmul(dst, lh, rh, start=False, stop=last)

            def queries0(i):
                pe.wait_ge(x_ready, i + 1)
                for c in range(C0):
                    if not (isinstance(i, int) and i == 0 and c < 2):
                        pe.wait_ge(q_ready, C0 * i + c - 1)
                    dst = A_BANKS[c % 2]
                    for k in range(KC):
                        cols = slice(c * P, (c + 1) * P)
                        last = split_product(dst[:], (wq0_hi[:, k, cols], wq0_lo[:, k, cols]),
                                             (x_hi[:, k, :], x_lo[:, k, :]), k == 0, k == KC - 1)
                    last.then_inc(q_psum_ready, 1)

            def logits0(i):
                for h in range(H0):
                    c, r = h // HC0, slice((h % HC0) * DK0, (h % HC0 + 1) * DK0)
                    if h % HC0 == 0:
                        pe.wait_ge(q_ready, C0 * i + c + 1)
                    if not (isinstance(i, int) and i == 0 and h < 3):
                        pe.wait_ge(masked_ready, H0 * i + max(h - 2, 0))
                    for b in range(B):
                        ks, qs = slice(b * KEYS, (b + 1) * KEYS), slice(b * QH, (b + 1) * QH)
                        last = split_product(B_BANKS[h_bank(h)][:, qs], (k0_hi[r, c, ks], k0_lo[r, c, ks]),
                                             (q0_hi[r, c, qs], q0_lo[r, c, qs]), True, True)
                    last.then_inc(logits_ready, 1)

            def values0(i):
                for c in range(C0):
                    if c % 2 == 0:
                        pe.wait_ge(probs_ready, HG * i + c // 2 + 1)
                    if not (isinstance(i, int) and i == 0 and c < 2):
                        pe.wait_ge(u_saved, (C0 + 1) * i + c - 1 - (0 if c >= 2 else 1))
                    for b in range(B):
                        for a in range(HC0):
                            h = HC0 * c + a
                            last = nc.tensor.matmul(U_BANKS[c % 2][a * DK0:(a + 1) * DK0, b * QH:(b + 1) * QH],
                                                    v0[:, b, h * DK0:(h + 1) * DK0],
                                                    scores[:, h, b * QH:(b + 1) * QH], start=True, stop=True)
                    last.then_inc(u_psum_ready, 1)
                if not (isinstance(i, int) and i == 0):
                    pe.wait_ge(u_saved, (C0 + 1) * i)
                row_sums(SUM_BANK).then_inc(sums_psum_ready, 1)

            def row_sums(dst):
                for j in range(HG):
                    for g in range(G):
                        last = nc.tensor.matmul(dst[32 * g:32 * g + 32, :], summer[:, j, :],
                                                scores[:, G * j + g, :], start=(j == 0), stop=(j == HG - 1))
                return last

            pe.wait_ge(wq0_ready, 1)
            queries0(0)
            logits0(0)
            queries0(1)
            values0(0)
            with pe.Fori(1, NB - 1) as i:
                logits0(i)
                queries0(i + 1)
                values0(i)
            logits0(NB - 1)
            values0(NB - 1)

            def spread(dst, sel, r, c):
                nc.tensor.matmul(dst, sel[:, c, :], r[1][:], start=True, stop=False)
                return nc.tensor.matmul(dst, sel[:, c, :], r[0][:], start=False, stop=True)

            def spread0(i, c):
                if c >= 2:
                    pe.wait_ge(attn0_ready, C0 * i + c - 1)
                spread(R_BANKS[c % 2][:], hs0, (r0_hi, r0_lo), c).then_inc(bc0_ready, 1)

            def output0(i, c):
                pe.wait_ge(a0_ready, C0 * i + c + 1)
                if isinstance(i, int) and i == 0:
                    pe.wait_ge(wo0_ready, c + 1)
                for t in range(QT):
                    ts = slice(t * P, (t + 1) * P)
                    last = split_product(Z_BANKS[t][:], (a0_hi[:, c % 2, ts], a0_lo[:, c % 2, ts]),
                                         (wo0_hi[:, c, :], wo0_lo[:, c, :]), c == 0, c == C0 - 1)
                last.then_inc(a0_used, 1)

            def values1(i):
                pe.wait_ge(probs1_ready, H1 * (i + 1))
                row_sums(R_BANKS[2]).then_inc(sums1_psum_ready, 1)
                for c in range(C1):
                    if c in (1, 2):
                        if not in_tail(i):
                            pe.wait_ge(attn0_ready, C0 * (i + 1) + C0 - 2 + c)
                    if c == 3:
                        pe.wait_ge(den1_ready, i + 1)
                    for b in range(B):
                        for a in range(HC1):
                            h = HC1 * c + a
                            last = nc.tensor.matmul(PV_BANKS[c][a * DK1:(a + 1) * DK1, b * QH:(b + 1) * QH],
                                                    v1[:, b, h * DK1:(h + 1) * DK1],
                                                    scores[:, h, b * QH:(b + 1) * QH], start=True, stop=True)
                    last.then_inc(u1_psum_ready, 1)

            def in_tail(i):
                return isinstance(i, int) and i == NB - 1

            def spread1(i):
                pe.wait_ge(r1_ready, i + 1)
                for c in range(C1):
                    pe.wait_ge(u1_saved, C1 * i + c + 1)
                    spread(PV_BANKS[c][:], hs1, (r1_hi, r1_lo), c).then_inc(bc1_ready, 1)

            def output1(i):
                for c in range(C1):
                    pe.wait_ge(a1_ready, C1 * i + c + 1)
                    for t in range(QT):
                        if c == 0 and not in_tail(i):
                            pe.wait_ge(z0_ready, QT * (i + 1) + t + 1)
                        ts = slice(t * P, (t + 1) * P)
                        last = split_product(Z_BANKS[t][:], (q1_hi[:, c, ts], q1_lo[:, c, ts]),
                                             (wo1_hi[:, c, :], wo1_lo[:, c, :]), c == 0, c == C1 - 1)
                last.then_inc(o1_ready, 1)

            def layer0_output(i, between):
                pe.wait_ge(r0_ready, i + 1)
                if not (isinstance(i, int) and i == 0):
                    pe.wait_ge(scores1_ready, H1 * i)
                spread0(i, 0)
                spread0(i, 1)
                for c in range(C0):
                    if c + 2 < C0:
                        spread0(i, c + 2)
                    if c == 5 and between:
                        values1(i - 1)
                    if c == 7 and between:
                        spread1(i - 1)
                    output0(i, c)

            def transposes(i):
                pe.wait_ge(n0_ready, QT * (i + 1))
                if isinstance(i, int) and i == 0:
                    pe.wait_ge(attn0_ready, C0)
                else:
                    pe.wait_ge(attn1_ready, C1 * i)
                for c in range(KC):
                    for t in range(QT):
                        last = nc.tensor.transpose(R_BANKS[c][:, t * P:(t + 1) * P],
                                                   z0[:, t, c * P:(c + 1) * P], ident[:])
                    last.then_inc(yt_psum_ready, 1)

            def queries1(i):
                pe.wait_ge(yt_ready, KC * (i + 1))
                for c in range(C1):
                    cols = slice(c * P, (c + 1) * P)
                    for k in range(KC):
                        last = split_product(R_BANKS[c][:], (wq1_hi[:, k, cols], wq1_lo[:, k, cols]),
                                             (yt_hi[:, k, :], yt_lo[:, k, :]), k == 0, k == KC - 1)
                    last.then_inc(q1_psum_ready, 1)

            def logits1(i):
                for c in range(C1):
                    banks = Z_BANKS if c % 2 == 0 else R_BANKS
                    pe.wait_ge(q1_ready, C1 * i + (c + 1 if c % 2 == 0 else C1))
                    if c == 0 and not (isinstance(i, int) and i == 0):
                        pe.wait_ge(z1_ready, QT * i)
                    if c == 0 and isinstance(i, int) and i == 0:
                        pe.wait_ge(z0_ready, QT)
                    for b in range(B):
                        ks, qs = slice(b * KEYS, (b + 1) * KEYS), slice(b * QH, (b + 1) * QH)
                        for n, (kk, qq) in enumerate(((k1_hi, q1_lo), (k1_lo, q1_hi), (k1_hi, q1_hi))):
                            for g in range(HC1):
                                if b == 0 and n == 0 and c >= 2:
                                    pe.wait_ge(scores1_ready, H1 * i + HC1 * (c - 2) + g + 1)
                                r = slice(g * DK1, (g + 1) * DK1)
                                last = nc.tensor.matmul(banks[g][:, qs], kk[r, c, ks], qq[r, c, qs],
                                                        start=(n == 0), stop=(n == 2))
                                if b == B - 1 and n == 2:
                                    last.then_inc(logits1_ready, 1)

            pe.wait_ge(u_saved, (C0 + 1) * NB)
            pe.wait_ge(hs_ready, 2)
            pe.wait_ge(consts_loaded, 16 * 11)
            layer0_output(0, False)
            pe.wait_ge(w1_loaded, 32)
            pe.wait_ge(attn0_ready, C0)
            for c in range(C1):
                for k in range(KC):
                    last = nc.tensor.matmul(R_BANKS[3][:, c:c + 1], s_stage[:, k * E1 + c * P:k * E1 + (c + 1) * P],
                                            b0_col[:, k:k + 1], start=(k == 0), stop=(k == KC - 1))
            last.then_inc(bq1_psum_ready, 1)
            pe.wait_ge(bq1_ready, 1)
            pe.wait_ge(w1_ready, 2)
            transposes(0)
            queries1(0)
            logits1(0)
            with pe.Fori(1, NB) as i:
                layer0_output(i, True)
                output1(i - 1)
                transposes(i)
                queries1(i)
                logits1(i)
            pe.wait_ge(scores1_ready, H1 * NB)
            values1(NB - 1)
            spread1(NB - 1)
            output1(NB - 1)

        @block.scalar
        def _(act):
            act.wait_ge(small_loaded, 64)
            for c in range(C0):
                act.wait_ge(kv_psum_ready, c + 1)
                nc.scalar.activation(k0_hi[:, c, :], bank[c][:, 0:B * KEYS], ACT.Identity,
                                     bias=bk_sb[:, c:c + 1]).then_inc(k_hi_ready, 1)
            first_k1 = C0 + B * E0 // 512
            for c in range(C1):
                act.wait_ge(kv_psum_ready, first_k1 + c + 1)
                nc.scalar.activation(k1_hi[:, c, :], bank[(first_k1 + c) % 8][:, 0:B * KEYS],
                                     ACT.Copy).then_inc(k_hi_ready, 1)
            act.wait_ge(setup_loaded[4], 16)
            nc.scalar.activation(wq0_hi[:].rearrange("p c n -> p (c n)"), w_stage[:],
                                 ACT.Copy).then_inc(wq0_hi_ready, 1)

            def x_high(i):
                act.wait_ge(x_loaded, 16 * (i + 1))
                if isinstance(i, int) and i == 0:
                    act.wait_ge(kv_done, C0 + C1 + B * (E0 + E1) // 512)
                else:
                    act.wait_ge(q_psum_ready, C0 * i)
                nc.scalar.activation(x_hi[:], x_raw[:], ACT.Copy).then_inc(x_hi_ready, 1)

            def mask_float(i):
                act.wait_ge(mask_loaded, 16 * (i + 1))
                if not (isinstance(i, int) and i == 0):
                    act.wait_ge(probs_ready, HG * i)
                nc.scalar.activation(mask_f[:], mask_raw[:], ACT.Copy).then_inc(mask_ready, 1)

            def q_high(i, c):
                act.wait_ge(q_psum_ready, C0 * i + c + 1)
                nc.scalar.activation(q0_hi[:, c, :], A_BANKS[c % 2][:], ACT.Identity,
                                     bias=bq_sb[:, c:c + 1]).then_inc(q_hi_ready, 1)

            def exponential(i, j):
                act.wait_ge(shift_ready, i + 1)
                four = scores[:, HG * j:HG * (j + 1), :]
                nc.scalar.activation(four, four, ACT.Exp, bias=neg_mx[:]).then_inc(exp_ready, 1)

            def save_u(i):
                if not (isinstance(i, int) and i == 0):
                    act.wait_ge(u_stored, 16 * i)
                    act.wait_ge(sums_stored, 16 * i)
                for c in range(C0):
                    act.wait_ge(u_psum_ready, C0 * i + c + 1)
                    nc.scalar.activation(u_out[:, c, :], U_BANKS[c % 2][:], ACT.Copy).then_inc(u_saved, 1)
                act.wait_ge(sums_psum_ready, i + 1)
                nc.scalar.activation(sums_out[:, 0:QB], SUM_BANK[:], ACT.Copy).then_inc(u_saved, 1)
                act.wait_ge(u_saved, (C0 + 1) * (i + 1))
                act.dma_start(at(u_dram, i), u_out[:].rearrange("p c n -> p (c n)")).then_inc(u_stored, 16)
                act.wait_ge(m_saved, i + 1)
                act.dma_start(at(sums_dram, i), sums_out[:]).then_inc(sums_stored, 16)

            def block1(i, more):
                if more:
                    x_high(i + 1)
                for c in range(C0):
                    if more:
                        q_high(i + 1, c)
                    if c < HG:
                        exponential(i, c)
                save_u(i)

            x_high(0)
            mask_float(0)
            for c in range(C0):
                q_high(0, c)
            block1(0, True)
            with act.Fori(1, NB - 1) as i:
                mask_float(i)
                block1(i, True)
            mask_float(NB - 1)
            block1(NB - 1, False)

            act.wait_ge(sums_psum_ready, NB)
            act.wait_ge(u_stored, 16 * NB)
            act.wait_ge(sums_stored, 16 * NB)
            act.wait_ge(probs_ready, HG * NB)
            act.wait_ge(q_ready, C0 * NB)

            def eps_factor(i, n):
                act.wait_ge(sums_loaded, 16 * (n + 1))
                if not (isinstance(n, int) and n == 0):
                    act.wait_ge(den0_ready, n)
                nc.scalar.activation(eps_f[:], sums_in[:, QB:QB + 1], ACT.Exp, bias=m_eps[:],
                                     scale=-1.0).then_inc(eps_ready, 1)

            act.wait_ge(m_eps_ready, 1)
            eps_factor(0, 0)
            act.wait_ge(wo0_loaded, 16)
            act.wait_ge(consts_loaded, 16 * 11)
            nc.scalar.activation(hs0[:].rearrange("p c n -> p (c n)"),
                                 sel0_raw, ACT.Copy).then_inc(hs_ready, 1)
            nc.scalar.activation(hs1[:].rearrange("p c n -> p (c n)"),
                                 sel1_raw, ACT.Copy).then_inc(hs_ready, 1)
            for c in range(C0):
                nc.scalar.activation(wo0_hi[:, c, :], w_stage[:, c * D:(c + 1) * D],
                                     ACT.Copy).then_inc(wo0_hi_ready, 1)

            def a0_high(i, c):
                act.wait_ge(attn0_ready, C0 * i + c + 1)
                if not (isinstance(i, int) and i == 0 and c < 2):
                    act.wait_ge(a0_used, C0 * i + c - 1)
                nc.scalar.activation(a0_hi[:, c % 2, :], u_in[:, c, :], ACT.Copy).then_inc(a0_hi_ready, 1)

            def save_u1(i):
                for c in range(C1):
                    act.wait_ge(u1_psum_ready, C1 * i + c + 1)
                    if c == 0 and not (isinstance(i, int) and i == 0):
                        act.wait_ge(a1_ready, C1 * i)
                    nc.scalar.activation(u1[:, c, :], PV_BANKS[c][:], ACT.Copy).then_inc(u1_saved, 1)

            def a1_high(i):
                for c in range(C1):
                    act.wait_ge(attn1_ready, C1 * i + c + 1)
                    nc.scalar.activation(q1_hi[:, c, :], u1[:, c, :], ACT.Copy).then_inc(a1_hi_ready, 1)

            def yt_high(i):
                for c in range(KC):
                    act.wait_ge(yt_psum_ready, KC * i + c + 1)
                    nc.scalar.activation(yt_hi[:, c, :], R_BANKS[c][:], ACT.Copy).then_inc(yt_hi_ready, 1)

            def q1_high(i):
                for c in range(C1):
                    act.wait_ge(q1_psum_ready, C1 * i + c + 1)
                    nc.scalar.activation(q1_hi[:, c, :], R_BANKS[c][:], ACT.Identity,
                                         bias=bq1_sb[:, c:c + 1]).then_inc(q1_hi_ready, 1)

            def exponential1(i):
                for h in range(H1):
                    if h % HC1 == 0:
                        act.wait_ge(shift1_ready, C1 * i + h // HC1 + 1)
                    nc.scalar.activation(scores[:, h, :], scores[:, h, :], ACT.Exp, bias=sh1[:, h:h + 1],
                                         scale=SCALE1).then_inc(probs1_ready, 1)

            def store_out(i):
                act.wait_ge(out_ready, QT * (i + 1))
                act.dma_start(at(out, i).rearrange("(t p) n -> p t n", p=P), z1[:]).then_inc(out_stored, 16)

            for c in range(C0):
                a0_high(0, c)
            act.wait_ge(w1_loaded, 32)
            for k in range(KC):
                nc.scalar.activation(wq1_hi[:, k, :], s_stage[:, k * E1:(k + 1) * E1], ACT.Copy,
                                     scale=g0_col[:, k:k + 1]).then_inc(w1_hi_ready, 1)
            nc.scalar.activation(wo1_hi[:].rearrange("p c n -> p (c n)"), s_stage[:, 2048:4096],
                                 ACT.Copy).then_inc(w1_hi_ready, 1)
            eps_factor(1, 1)
            act.wait_ge(w1_ready, 2)
            act.wait_ge(bq1_ready, 1)
            yt_high(0)
            q1_high(0)
            exponential1(0)
            with act.Fori(1, NB) as i:
                for c in range(5):
                    a0_high(i, c)
                save_u1(i - 1)
                for c in range(5, C0):
                    a0_high(i, c)
                a1_high(i - 1)
                eps_factor(i + 1, i + 1)
                yt_high(i)
                q1_high(i)
                exponential1(i)
                store_out(i - 1)
            save_u1(NB - 1)
            a1_high(NB - 1)
            store_out(NB - 1)

        @block.vector
        def _(dve):
            def f(ap):
                return ap.bitcast(f32)

            dve.wait_ge(small_loaded, 64)
            for c in range(C0):
                dve.wait_ge(k_hi_ready, c + 1)
                nc.vector.scalar_tensor_tensor(out=k0_lo[:, c, :], in0=bank[c][:, 0:B * KEYS],
                                               scalar=bk_sb[:, c:c + 1], in1=f(k0_hi[:, c, :]),
                                               op0=ALU.add, op1=ALU.subtract).then_inc(kv_done, 1)
            n = C0
            for b in range(B):
                for half in range(E0 // 512):
                    dve.wait_ge(kv_psum_ready, n + 1)
                    cols = slice(half * 512, (half + 1) * 512)
                    nc.vector.tensor_tensor(v0[:, b, cols], bank[n % 8][:], bv_sb[:, cols], ALU.add).then_inc(kv_done, 1)
                    n += 1
            for c in range(C1):
                dve.wait_ge(k_hi_ready, C0 + c + 1)
                nc.vector.tensor_tensor(k1_lo[:, c, :], bank[n % 8][:, 0:B * KEYS], f(k1_hi[:, c, :]),
                                        ALU.subtract).then_inc(kv_done, 1)
                n += 1
            for b in range(B):
                dve.wait_ge(kv_psum_ready, n + 1)
                nc.vector.tensor_copy(v1[:, b, :], bank[n % 8][:]).then_inc(kv_done, 1)
                n += 1
            dve.wait_ge(wq0_hi_ready, 1)
            nc.vector.tensor_tensor(wq0_lo[:].rearrange("p c n -> p (c n)"), w_stage[:],
                                    f(wq0_hi[:]).rearrange("p c n -> p (c n)"), ALU.subtract).then_inc(wq0_ready, 1)

            def x_low(i):
                dve.wait_ge(x_hi_ready, i + 1)
                nc.vector.tensor_tensor(x_lo[:], x_raw[:], f(x_hi[:]), ALU.subtract).then_inc(x_ready, 1)

            def q_low(i, c):
                dve.wait_ge(q_hi_ready, C0 * i + c + 1)
                nc.vector.scalar_tensor_tensor(out=q0_lo[:, c, :], in0=A_BANKS[c % 2][:],
                                               scalar=bq_sb[:, c:c + 1], in1=f(q0_hi[:, c, :]),
                                               op0=ALU.add, op1=ALU.subtract).then_inc(q_ready, 1)

            def mask_scores(i):
                dve.wait_ge(mask_ready, i + 1)
                for h in range(H0):
                    dve.wait_ge(logits_ready, H0 * i + h + 1)
                    nc.vector.nop(nofuse=True)
                    nc.vector.tensor_tensor_reduce(out=scores[:, h, :], in0=B_BANKS[h_bank(h)][:], in1=mask_f[:],
                                                   scale=1.0, scalar=-3e38, op0=ALU.mult, op1=ALU.max,
                                                   accum_out=maxes[:, h:h + 1]).then_inc(masked_ready, 1)

            def running_max(i):
                dve.wait_ge(masked_ready, H0 * (i + 1))
                nc.vector.reduce_max(tile_mx[:], maxes[:], AX.X).then_inc(tile_max_ready, 1)
                dve.wait_ge(all_max_ready, i + 1)
                if isinstance(i, int) and i == 0:
                    nc.vector.tensor_copy(run_max[:], all_mx[:]).then_inc(run_max_ready, 1)
                else:
                    nc.vector.tensor_tensor(run_max[:], run_max[:], all_mx[:], ALU.max).then_inc(run_max_ready, 1)
                dve.wait_ge(run_max_ready, i + 1)
                nc.vector.tensor_scalar(neg_mx[:], run_max[:], -1.0, None, ALU.mult).then_inc(shift_ready, 1)
                if not (isinstance(i, int) and i == 0):
                    dve.wait_ge(sums_stored, 16 * i)
                nc.vector.tensor_scalar(sums_out[:, QB:SUMW], run_max[:].to_broadcast([P, SUMW - QB]),
                                        1.0, None, ALU.mult).then_inc(m_saved, 1)

            def mask_probs(i, j):
                dve.wait_ge(exp_ready, HG * i + j + 1)
                four = scores[:, HG * j:HG * (j + 1), :]
                nc.vector.tensor_tensor(four, four, mask_f[:].unsqueeze(1).to_broadcast([P, HG, QB]),
                                        ALU.mult).then_inc(probs_ready, 1)

            def block1(i, more):
                mask_scores(i)
                running_max(i)
                if more:
                    x_low(i + 1)
                for c in range(C0):
                    if more:
                        q_low(i + 1, c)
                    if 1 <= c <= HG:
                        mask_probs(i, c - 1)

            x_low(0)
            for c in range(C0):
                q_low(0, c)
            block1(0, True)
            with dve.Fori(1, NB - 1) as i:
                block1(i, True)
            block1(NB - 1, False)

            dve.wait_ge(sums_psum_ready, NB)
            dve.wait_ge(u_stored, 16 * NB)
            dve.wait_ge(sums_stored, 16 * NB)
            dve.wait_ge(m_saved, NB)
            nc.vector.tensor_scalar(m_eps[:], run_max[:], math.log(SUM_EPS), None, ALU.add).then_inc(m_eps_ready, 1)
            nc.vector.memset(mhalf[:], -0.5).then_inc(mhalf_ready, 1)

            def reciprocals0(n):
                dve.wait_ge(eps_ready, n + 1)
                nc.vector.tensor_scalar(den[:], sums_in[:, 0:QB], eps_f[:], None, ALU.add).then_inc(den0_ready, 1)
                dve.wait_ge(den0_ready, n + 1)
                nc.vector.reciprocal(den[:], den[:]).then_inc(rec0_ready, 1)
                dve.wait_ge(rec0_ready, n + 1)
                nc.vector.tensor_copy(r0_hi[:], den[:]).then_inc(r0_hi_ready, 1)
                dve.wait_ge(r0_hi_ready, n + 1)
                nc.vector.tensor_tensor(r0_lo[:], den[:], f(r0_hi[:]), ALU.subtract).then_inc(r0_ready, 1)

            reciprocals0(0)
            for c in range(C0):
                dve.wait_ge(wo0_hi_ready, c + 1)
                nc.vector.tensor_tensor(wo0_lo[:, c, :], w_stage[:, c * D:(c + 1) * D], f(wo0_hi[:, c, :]),
                                        ALU.subtract).then_inc(wo0_ready, 1)

            def attention0(i):
                dve.wait_ge(u_loaded, 16 * (i + 1))
                for c in range(C0):
                    dve.wait_ge(bc0_ready, C0 * i + c + 1)
                    nc.vector.tensor_tensor(u_in[:, c, :], u_in[:, c, :], R_BANKS[c % 2][:],
                                            ALU.mult).then_inc(attn0_ready, 1)

            def reciprocals1(i):
                dve.wait_ge(sums1_psum_ready, i + 1)
                nc.vector.tensor_scalar(den[:], R_BANKS[2][:], 1e-36, None, ALU.max).then_inc(den1_ready, 1)
                dve.wait_ge(den1_ready, i + 1)
                nc.vector.reciprocal(den[:], den[:]).then_inc(rec1_ready, 1)
                dve.wait_ge(rec1_ready, i + 1)
                nc.vector.tensor_copy(r1_hi[:], den[:]).then_inc(r1_hi_ready, 1)
                dve.wait_ge(r1_hi_ready, i + 1)
                nc.vector.tensor_tensor(r1_lo[:], den[:], f(r1_hi[:]), ALU.subtract).then_inc(r1_ready, 1)

            def attention1(i):
                for c in range(C1):
                    dve.wait_ge(bc1_ready, C1 * i + c + 1)
                    nc.vector.tensor_tensor(u1[:, c, :], u1[:, c, :], PV_BANKS[c][:],
                                            ALU.mult).then_inc(attn1_ready, 1)

            def rows0(i):
                dve.wait_ge(a0_used, C0 * (i + 1))
                dve.wait_ge(xb_ready, i + 1)
                for t in range(QT):
                    nc.vector.tensor_tensor(z0[:, t, :], Z_BANKS[t][:], z0[:, t, :], ALU.add).then_inc(z0_ready, 1)
                for t in range(QT):
                    dve.wait_ge(z0_ready, QT * i + t + 1)
                    nc.vector.bn_stats(st0[:, t, :], z0[:, t, :]).then_inc(bn0_ready, 1)
                for t in range(QT):
                    dve.wait_ge(bn0_ready, QT * i + t + 1)
                    nc.vector.nop(nofuse=True)
                    nc.vector.bn_aggr(mv0[:, t, :], st0[:, t, :]).then_inc(mv0_ready, 1)

            def norm0(i):
                dve.wait_ge(rstd0_ready, i + 1)
                for t in range(QT):
                    nc.vector.tensor_scalar(z0[:, t, :], z0[:, t, :], mv0[:, t, 0:1], rs0[:, t:t + 1],
                                            ALU.subtract, ALU.mult).then_inc(n0_ready, 1)

            def yt_low(i):
                for c in range(KC):
                    dve.wait_ge(yt_hi_ready, KC * i + c + 1)
                    nc.vector.tensor_tensor(yt_lo[:, c, :], R_BANKS[c][:], f(yt_hi[:, c, :]),
                                            ALU.subtract).then_inc(yt_ready, 1)

            def q1_low(i):
                for c in range(C1):
                    dve.wait_ge(q1_hi_ready, C1 * i + c + 1)
                    nc.vector.scalar_tensor_tensor(out=q1_lo[:, c, :], in0=R_BANKS[c][:], scalar=bq1_sb[:, c:c + 1],
                                                   in1=f(q1_hi[:, c, :]), op0=ALU.add,
                                                   op1=ALU.subtract).then_inc(q1_ready, 1)

            def scores_and_max1(i):
                for h in range(H1):
                    c, g = h // HC1, h % HC1
                    dve.wait_ge(logits1_ready, H1 * i + h + 1)
                    nc.vector.tensor_scalar(scores[:, h, :], (Z_BANKS if c % 2 == 0 else R_BANKS)[g][:], 1.0, -3e38,
                                            ALU.mult, ALU.max, accum_out=mx1[:, h:h + 1]).then_inc(scores1_ready, 1)
                    if g == HC1 - 1 and c >= 1:
                        shift1(i, c - 1)
                shift1(i, C1 - 1)

            def shift1(i, c):
                dve.wait_ge(amax1_ready, C1 * i + c + 1)
                hs = slice(HC1 * c, HC1 * (c + 1))
                nc.vector.tensor_scalar(sh1[:, hs], amx1[:, hs], -SCALE1, HEADROOM, ALU.mult,
                                        ALU.add).then_inc(shift1_ready, 1)

            def rows1(i):
                dve.wait_ge(o1_ready, i + 1)
                dve.wait_ge(resid_ready, i + 1)
                if not (isinstance(i, int) and i == 0):
                    dve.wait_ge(out_stored, 16 * i)
                for t in range(QT):
                    nc.vector.tensor_tensor(z1[:, t, :], Z_BANKS[t][:], resid[:, t, :], ALU.add).then_inc(z1_ready, 1)
                for t in range(QT):
                    dve.wait_ge(z1_ready, QT * i + t + 1)
                    nc.vector.bn_stats(st1[:, t, :], z1[:, t, :]).then_inc(bn1_ready, 1)
                for t in range(QT):
                    dve.wait_ge(bn1_ready, QT * i + t + 1)
                    nc.vector.nop(nofuse=True)
                    nc.vector.bn_aggr(mv1[:, t, :], st1[:, t, :]).then_inc(mv1_ready, 1)

            def norm1(i):
                dve.wait_ge(rstd1_ready, i + 1)
                for t in range(QT):
                    nc.vector.scalar_tensor_tensor(out=z1[:, t, :], in0=z1[:, t, :], scalar=mv1[:, t, 0:1],
                                                   in1=g1_b[:], op0=ALU.subtract, op1=ALU.mult).then_inc(ng1_ready, 1)
                for t in range(QT):
                    dve.wait_ge(ng1_ready, QT * i + t + 1)
                    nc.vector.scalar_tensor_tensor(out=z1[:, t, :], in0=z1[:, t, :], scalar=rs1[:, t:t + 1],
                                                   in1=be1_b[:], op0=ALU.mult, op1=ALU.add).then_inc(out_ready, 1)

            attention0(0)
            for k in range(KC):
                dve.wait_ge(w1_hi_ready, k + 1)
                last = nc.vector.scalar_tensor_tensor(out=wq1_lo[:, k, :], in0=s_stage[:, k * E1:(k + 1) * E1],
                                                      scalar=g0_col[:, k:k + 1], in1=f(wq1_hi[:, k, :]),
                                                      op0=ALU.mult, op1=ALU.subtract)
            last.then_inc(w1_ready, 1)
            dve.wait_ge(w1_hi_ready, KC + 1)
            nc.vector.tensor_tensor(wo1_lo[:].rearrange("p c n -> p (c n)"), s_stage[:, 2048:4096],
                                    f(wo1_hi[:]).rearrange("p c n -> p (c n)"), ALU.subtract).then_inc(w1_ready, 1)
            dve.wait_ge(bq1_psum_ready, 1)
            nc.vector.tensor_copy(bq1_sb[:], R_BANKS[3][:, 0:C1]).then_inc(bq1_ready, 1)
            rows0(0)
            reciprocals0(1)
            norm0(0)
            yt_low(0)
            q1_low(0)
            scores_and_max1(0)
            with dve.Fori(1, NB) as i:
                attention0(i)
                reciprocals1(i - 1)
                attention1(i - 1)
                rows0(i)
                norm0(i)
                reciprocals0(i + 1)
                rows1(i - 1)
                yt_low(i)
                q1_low(i)
                norm1(i - 1)
                scores_and_max1(i)
            reciprocals1(NB - 1)
            attention1(NB - 1)
            rows1(NB - 1)
            norm1(NB - 1)

        @block.gpsimd
        def _(pool):
            def f(ap):
                return ap.bitcast(f32)

            def all_max(i):
                pool.wait_ge(tile_max_ready, i + 1)
                nc.gpsimd.nop(nofuse=True)
                nc.gpsimd.partition_all_reduce(all_mx[:], tile_mx[:], P, MAX).then_inc(all_max_ready, 1)

            all_max(0)
            with pool.Fori(1, NB) as i:
                all_max(i)

            def a0_low(i):
                for c in range(C0):
                    pool.wait_ge(a0_hi_ready, C0 * i + c + 1)
                    nc.gpsimd.tensor_tensor(a0_lo[:, c % 2, :], u_in[:, c, :], f(a0_hi[:, c % 2, :]),
                                            ALU.subtract).then_inc(a0_ready, 1)

            def a1_low(i):
                for c in range(C1):
                    pool.wait_ge(a1_hi_ready, C1 * i + c + 1)
                    nc.gpsimd.tensor_tensor(q1_lo[:, c, :], u1[:, c, :], f(q1_hi[:, c, :]),
                                            ALU.subtract).then_inc(a1_ready, 1)

            def x_and_bias(i):
                pool.wait_ge(xn_loaded, 16 * (i + 1))
                nc.gpsimd.tensor_tensor(z0[:], z0[:], bo0_b[:].unsqueeze(1).to_broadcast([P, QT, D]),
                                        ALU.add).then_inc(xb_ready, 1)

            def rstd(i, mv, rs, mv_ready, var_ready, rstd_ready):
                pool.wait_ge(mv_ready, QT * (i + 1))
                nc.gpsimd.nop(nofuse=True)
                nc.gpsimd.tensor_scalar(rs[:], mv[:, :, 1], LN_EPS, 1.0, ALU.add, ALU.mult).then_inc(var_ready, 1)
                pool.wait_ge(var_ready, i + 1)
                nc.gpsimd.tensor_tensor(rs[:], rs[:], mhalf[:], ALU.pow).then_inc(rstd_ready, 1)

            def residual1(i):
                if not (isinstance(i, int) and i == 0):
                    pool.wait_ge(z1_ready, QT * i)
                pool.wait_ge(n0_ready, QT * (i + 1))
                nc.gpsimd.tensor_tensor(resid[:], z0[:], g0_b[:].unsqueeze(1).to_broadcast([P, QT, D]),
                                        ALU.mult).then_inc(rg_ready, 1)
                pool.wait_ge(rg_ready, i + 1)
                nc.gpsimd.tensor_tensor(resid[:], resid[:], bb1_b[:].unsqueeze(1).to_broadcast([P, QT, D]),
                                        ALU.add).then_inc(resid_ready, 1)

            def head_max(i):
                for c in range(C1):
                    pool.wait_ge(scores1_ready, H1 * i + HC1 * (c + 1))
                    nc.gpsimd.nop(nofuse=True)
                    hs = slice(HC1 * c, HC1 * (c + 1))
                    nc.gpsimd.partition_all_reduce(amx1[:, hs], mx1[:, hs], P, MAX).then_inc(amax1_ready, 1)

            pool.wait_ge(consts_loaded, 16 * 11)
            nc.gpsimd.tensor_tensor(bb1_b[:], bb1_b[:], beta0_b, ALU.add).then_inc(bb1_ready, 1)
            x_and_bias(0)
            a0_low(0)
            pool.wait_ge(mhalf_ready, 1)
            rstd(0, mv0, rs0, mv0_ready, var0_ready, rstd0_ready)
            pool.wait_ge(hs_ready, 2)
            pool.wait_ge(bb1_ready, 1)
            residual1(0)
            head_max(0)
            with pool.Fori(1, NB) as i:
                x_and_bias(i)
                a0_low(i)
                a1_low(i - 1)
                rstd(i, mv0, rs0, mv0_ready, var0_ready, rstd0_ready)
                rstd(i - 1, mv1, rs1, mv1_ready, var1_ready, rstd1_ready)
                residual1(i)
                head_max(i)
            a1_low(NB - 1)
            rstd(NB - 1, mv1, rs1, mv1_ready, var1_ready, rstd1_ready)


def h_bank(h):
    return h % 3


def kernel(x, ctx_1024, mask_BxSxS2_ik1, L0_xattn_Wq, L0_xattn_bq, L0_xattn_Wk, L0_xattn_bk, L0_xattn_Wv,
           L0_xattn_bv, L0_xattn_Wo, L0_xattn_bo, L0_xattn_gamma, L0_xattn_beta, L1_xattn_Wq, L1_xattn_Wk,
           L1_xattn_Wv, L1_xattn_Wo, L1_xattn_bo, L1_xattn_ln_gamma, L1_xattn_ln_beta):
    import concourse.bacc as bacc
    from concourse.bass_utils import run_bass_kernel_spmd

    def blocks(a, last):
        return np.asarray(a).reshape(B, NB, QH, last).transpose(1, 0, 2, 3).reshape(NB, QB, last)

    xb = blocks(x, D)
    mask = blocks(mask_BxSxS2_ik1, KEYS)
    sum_sel = np.zeros((P, HG, 32), np.float32)
    for j in range(HG):
        sum_sel[:, j, j] = 1

    def head_sel(chunks, width):
        sel = np.zeros((P, chunks, P), np.float32)
        for c in range(chunks):
            for p in range(P):
                h = (c * P + p) // width
                sel[32 * (h % G) + h // G, c, p] = 1
        return sel.reshape(P, chunks * P)

    def columns(v, chunks):
        return np.asarray(v).reshape(chunks, P).T

    arrays = {
        "x_t": xb.transpose(0, 2, 1), "x_n": xb, "mask_t": mask.transpose(0, 2, 1),
        "ctx_t": np.asarray(ctx_1024).reshape(B * KEYS, D).T,
        "wq0": L0_xattn_Wq, "wk0": L0_xattn_Wk, "wv0": L0_xattn_Wv, "wo0": L0_xattn_Wo,
        "wq1": np.asarray(L1_xattn_Wq).T, "wk1": np.asarray(L1_xattn_Wk).T,
        "wv1": np.asarray(L1_xattn_Wv).T, "wo1": np.asarray(L1_xattn_Wo).T,
        "bq0": columns(L0_xattn_bq, C0), "bk0": columns(L0_xattn_bk, C0), "bv0": L0_xattn_bv,
        "bo0": L0_xattn_bo, "gamma0": L0_xattn_gamma, "beta0": L0_xattn_beta,
        "gcol0": columns(L0_xattn_gamma, KC), "bcol0": columns(L0_xattn_beta, KC),
        "bo1": L1_xattn_bo, "gamma1": L1_xattn_ln_gamma, "beta1": L1_xattn_ln_beta,
        "sum_sel": sum_sel, "head_sel0": head_sel(C0, DK0), "head_sel1": head_sel(C1, DK1),
        "identity": np.eye(P, dtype=np.float32),
    }
    arrays = {k: np.ascontiguousarray(v) for k, v in arrays.items()}
    nc = bacc.Bacc("TRN2", target_bir_lowering=False, num_devices=1, dynamic_dma_scratch_size=4096)
    args = [nc.dram_tensor(k, a.shape, mybir.dt.from_np(a.dtype), kind="ExternalInput").ap()
            for k, a in arrays.items()]
    out = nc.dram_tensor("out", (NB, QB, D), mybir.dt.float32, kind="ExternalOutput").ap()
    cross_attention_program(nc, *args, out)
    r = run_bass_kernel_spmd(nc, [arrays], core_ids=[0])
    return np.asarray(r.results[0]["out"]).reshape(NB, B, QH, D).transpose(1, 0, 2, 3).reshape(B, S, D)
```

```python
import math
from contextlib import ExitStack

import numpy as np

import concourse.bass as bass
from concourse import mybir

P = 128
B, S, D, KEYS = 2, 2048, 512, 128
H0, DK0 = 16, 64
H1, DK1 = 16, 32
E0, E1 = H0 * DK0, H1 * DK1
QB = 512
QH = QB // B
NB = B * S // QB
QT = QB // P
KC = D // P
C0, C1 = E0 // P, E1 // P
HC0, HC1 = P // DK0, P // DK1
G = 4
HG = H0 // G
LN_EPS = 1e-5
SUM_EPS = 1e-15
SCALE1 = 1.0 / math.sqrt(DK1)
HEADROOM = 40.0
SUMW = QB + 8


def cross_attention_program(nc, x_t, x_n, mask_t, ctx_t, wq0, wk0, wv0, wo0, wq1, wk1, wv1, wo1,
                            bq0, bk0, bv0, bo0, gamma0, beta0, gcol0, bcol0, bo1, gamma1, beta1,
                            sum_sel, head_sel0, head_sel1, identity, out):
    f32, f32r, i32 = mybir.dt.float32, mybir.dt.float32r, mybir.dt.int32
    ALU, ACT, AX = mybir.AluOpType, mybir.ActivationFunctionType, mybir.AxisListType
    MAX = bass.bass_isa.ReduceOp.max

    u_dram = nc.dram_tensor("u_dram", [NB, P, C0 * QB], f32, kind="Internal").ap()
    sums_dram = nc.dram_tensor("sums_dram", [NB, P, SUMW], f32, kind="Internal").ap()

    def at(dram, i):
        return dram[i] if isinstance(i, int) else dram[bass.ds(i, 1)].rearrange("a p n -> (a p) n")

    with ExitStack() as ctx:
        def sb(stack, name, shape, dt=f32):
            return stack.enter_context(nc.sbuf_tensor(name, shape, dt))

        def sem(name):
            return ctx.enter_context(nc.semaphore(name))

        def region(kib, *layouts):
            for layout in layouts:
                with ExitStack() as stack:
                    layout(stack)
            sb(ctx, f"region{len(regions)}", [P, kib * 256])
            regions.append(kib)

        regions, t = [], {}

        def put(stack, names, shape, dt=f32):
            for name in names.split():
                t[name] = sb(stack, name, shape, dt)

        put(ctx, "k1_hi k1_lo", [P, C1, B * KEYS], f32r)
        put(ctx, "v1", [P, B, E1])
        put(ctx, "summer", [P, HG, 32])
        put(ctx, "hs0", [P, C0, P], f32r)
        put(ctx, "hs1", [P, C1, P], f32r)
        put(ctx, "ident", [P, P])
        put(ctx, "bo0_b g0_b bb1_b g1_b be1_b", [P, D])
        put(ctx, "g0_col b0_col", [P, KC])
        put(ctx, "bq_sb bk_sb", [P, C0])
        put(ctx, "bq1_sb", [P, C1])
        put(ctx, "maxes mx1 amx1 sh1", [P, H0])
        put(ctx, "run_max tile_mx all_mx neg_mx eps_f m_eps", [P, 1])
        put(ctx, "st0 st1", [P, QT, 6])
        put(ctx, "mv0 mv1", [P, QT, 2])
        put(ctx, "rs0 rs1 mhalf", [P, QT])
        region(16, lambda k: put(k, "w_stage", [P, 4096]), lambda k: put(k, "resid z1", [P, QT, D]))
        region(32, lambda k: put(k, "yt_hi yt_lo", [P, KC, QB], f32r), lambda k: put(k, "scores", [P, H0, QB]))
        region(32, lambda k: put(k, "wq0_hi wq0_lo", [P, KC, E0], f32r),
               lambda k: put(k, "wo0_hi wo0_lo", [P, C0, D], f32r))
        region(24, lambda k: (put(k, "x_hi x_lo", [P, KC, QB], f32r), put(k, "x_raw", [P, KC, QB])),
               lambda k: (put(k, "wk1_sb wv1_sb", [P, KC, E1]), put(k, "ctx1_sb", [P, KC, B * KEYS])),
               lambda k: (put(k, "a_hi a_lo", [P, 2, QB], f32r), put(k, "q1_hi q1_lo", [P, C1, QB], f32r)))
        region(37, lambda k: (put(k, "wk0_sb wv0_sb", [P, KC, E0]), put(k, "ctx_sb", [P, KC, B * KEYS])),
               lambda k: put(k, "q0_hi q0_lo", [P, C0, QB], f32r),
               lambda k: (put(k, "u_in", [P, C0, QB]), put(k, "xn", [P, QT, D]), put(k, "sums_in", [P, SUMW]),
                          put(k, "den", [P, QB]), put(k, "r0_hi r0_lo r1_hi r1_lo", [P, QB], f32r)))
        region(40, lambda k: (put(k, "k0_hi k0_lo", [P, C0, B * KEYS], f32r), put(k, "v0", [P, B, E0]),
                              put(k, "u_out", [P, C0, QB])),
               lambda k: (put(k, "_keys_values_0", [P, 24 * 256]), put(k, "bv_sb", [P, E0])),
               lambda k: (put(k, "wq1_hi wq1_lo", [P, KC, E1], f32r), put(k, "wo1_hi wo1_lo", [P, C1, D], f32r),
                          put(k, "u1", [P, C1, QB])))
        region(8, lambda k: (put(k, "mask_raw", [P, QB], i32), put(k, "mask_f", [P, QB]),
                             put(k, "sums_out", [P, SUMW])),
               lambda k: put(k, "z0", [P, QT, D]))
        (k1_hi, k1_lo, v1, summer, hs0, hs1, ident) = (t[n] for n in "k1_hi k1_lo v1 summer hs0 hs1 ident".split())
        bo0_b, g0_b, bb1_b, g1_b, be1_b, g0_col, b0_col, bq_sb, bk_sb = (t[n] for n in "bo0_b g0_b bb1_b g1_b be1_b g0_col b0_col bq_sb bk_sb".split())
        bq1_sb, maxes, mx1, amx1, sh1, run_max, tile_mx, all_mx, neg_mx = (t[n] for n in "bq1_sb maxes mx1 amx1 sh1 run_max tile_mx all_mx neg_mx".split())
        eps_f, m_eps, st0, st1, mv0, mv1, rs0, rs1, mhalf = (t[n] for n in "eps_f m_eps st0 st1 mv0 mv1 rs0 rs1 mhalf".split())
        w_stage, resid, z1, yt_hi, yt_lo, scores, wq0_hi, wq0_lo, wo0_hi = (t[n] for n in "w_stage resid z1 yt_hi yt_lo scores wq0_hi wq0_lo wo0_hi".split())
        wo0_lo, x_hi, x_lo, x_raw, wk1_sb, wv1_sb, ctx1_sb, a_hi, a_lo = (t[n] for n in "wo0_lo x_hi x_lo x_raw wk1_sb wv1_sb ctx1_sb a_hi a_lo".split())
        q1_hi, q1_lo, wk0_sb, wv0_sb, ctx_sb, q0_hi, q0_lo, u_in, xn = (t[n] for n in "q1_hi q1_lo wk0_sb wv0_sb ctx_sb q0_hi q0_lo u_in xn".split())
        sums_in, den, r0_hi, r0_lo, k0_hi, k0_lo, v0, u_out, bv_sb = (t[n] for n in "sums_in den r0_hi r0_lo k0_hi k0_lo v0 u_out bv_sb".split())
        wq1_hi, wq1_lo, wo1_hi, wo1_lo, u1, mask_raw, mask_f, sums_out, z0 = (t[n] for n in "wq1_hi wq1_lo wo1_hi wo1_lo u1 mask_raw mask_f sums_out z0".split())
        r1_hi, r1_lo = (t[n] for n in "r1_hi r1_lo".split())
        sel0_raw, sel1_raw = w_stage[:, 0:C0 * P], w_stage[:, C0 * P:(C0 + C1) * P]
        beta0_b = w_stage[:, (C0 + C1) * P:(C0 + C1) * P + D]
        s_stage = scores[:, 0:8, :].rearrange("p h n -> p (h n)")

        bank = [ctx.enter_context(nc.psum_tensor(f"bank{n}", [P, 512], f32)) for n in range(8)]
        A_BANKS, B_BANKS, U_BANKS, SUM_BANK = bank[0:2], bank[2:5], bank[5:7], bank[7]
        Z_BANKS, R_BANKS = bank[0:4], bank[4:8]
        PV_BANKS, SUM1_BANK = [R_BANKS[3], R_BANKS[0], R_BANKS[1], R_BANKS[2]], R_BANKS[2]

        k0_loaded, v0_loaded, wq0_loaded, kv1_loaded = (sem(n) for n in (
            "k0_loaded", "v0_loaded", "wq0_loaded", "kv1_loaded"))
        small_loaded = sem("small_loaded")
        x_loaded, mask_loaded = sem("x_loaded"), sem("mask_loaded")
        u_stored, sums_stored = sem("u_stored"), sem("sums_stored")
        wo0_loaded, w1_loaded, consts_loaded, sel_loaded = (sem(n) for n in (
            "wo0_loaded", "w1_loaded", "consts_loaded", "sel_loaded"))
        u_loaded, sums_loaded, xn_loaded, out_stored = (sem(n) for n in (
            "u_loaded", "sums_loaded", "xn_loaded", "out_stored"))
        kv_psum_ready, k_hi_ready, kv_done, wq0_hi_ready, wq0_ready = (sem(n) for n in (
            "kv_psum_ready", "k_hi_ready", "kv_done", "wq0_hi_ready", "wq0_ready"))
        kv1_psum_ready, k1_hi_ready, kv1_done = (sem(n) for n in ("kv1_psum_ready", "k1_hi_ready", "kv1_done"))
        x_hi_ready, x_ready = sem("x_hi_ready"), sem("x_ready")
        mask_ready = sem("mask_ready")
        q_psum_ready, q_hi_ready, q_ready = sem("q_psum_ready"), sem("q_hi_ready"), sem("q_ready")
        logits_ready, masked_ready = sem("logits_ready"), sem("masked_ready")
        tile_max_ready, all_max_ready, run_max_ready, shift_ready, m_saved = (sem(n) for n in (
            "tile_max_ready", "all_max_ready", "run_max_ready", "shift_ready", "m_saved"))
        exp_ready, probs_ready = sem("exp_ready"), sem("probs_ready")
        u_psum_ready, sums_psum_ready = sem("u_psum_ready"), sem("sums_psum_ready")
        u_saved = sem("u_saved")
        m_eps_ready, mhalf_ready, wo0_hi_ready, wo0_ready, w1_hi_ready, w1_ready, hs_ready, bb1_ready = (
            sem(n) for n in ("m_eps_ready", "mhalf_ready", "wo0_hi_ready", "wo0_ready", "w1_hi_ready",
                             "w1_ready", "hs_ready", "bb1_ready"))
        bq1_psum_ready, bq1_ready = sem("bq1_psum_ready"), sem("bq1_ready")
        eps_ready, den0_ready, rec0_ready, r0_hi_ready, r0_ready = (sem(n) for n in (
            "eps_ready", "den0_ready", "rec0_ready", "r0_hi_ready", "r0_ready"))
        bc0_ready, attn0_ready, a0_hi_ready, a0_ready = (sem(n) for n in (
            "bc0_ready", "attn0_ready", "a0_hi_ready", "a0_ready"))
        a0_used, a1_used = sem("a0_used"), sem("a1_used")
        o0_ready, o1_ready = sem("o0_ready"), sem("o1_ready")
        xb_ready = sem("xb_ready")
        z0_ready, bn0_ready, mv0_ready, n0_ready = (sem(n) for n in (
            "z0_ready", "bn0_ready", "mv0_ready", "n0_ready"))
        var0_ready, rstd0_ready = sem("var0_ready"), sem("rstd0_ready")
        rg_ready, resid_ready = sem("rg_ready"), sem("resid_ready")
        yt_psum_ready, yt_hi_ready, yt_ready = (sem(n) for n in (
            "yt_psum_ready", "yt_hi_ready", "yt_ready"))
        q1_psum_ready, q1_hi_ready, q1_ready = (sem(n) for n in (
            "q1_psum_ready", "q1_hi_ready", "q1_ready"))
        logits1_ready, scores1_ready = sem("logits1_ready"), sem("scores1_ready")
        amax1_ready, shift1_ready = sem("amax1_ready"), sem("shift1_ready")
        probs1_ready = sem("probs1_ready")
        sums1_psum_ready, sums1_saved, den1_ready, rec1_ready, r1_hi_ready, r1_ready = (sem(n) for n in (
            "sums1_psum_ready", "sums1_saved", "den1_ready", "rec1_ready", "r1_hi_ready", "r1_ready"))
        u1_psum_ready, u1_saved, bc1_ready, attn1_ready, a1_hi_ready, a1_ready = (sem(n) for n in (
            "u1_psum_ready", "u1_saved", "bc1_ready", "attn1_ready", "a1_hi_ready", "a1_ready"))
        z1_ready, bn1_ready, mv1_ready, ng1_ready, out_ready = (sem(n) for n in (
            "z1_ready", "bn1_ready", "mv1_ready", "ng1_ready", "out_ready"))
        var1_ready, rstd1_ready = sem("var1_ready"), sem("rstd1_ready")

        block = ctx.enter_context(nc.Block())

        def upto(i, n):
            return isinstance(i, int) and i <= n

        @block.sync
        def _(sp):
            def chunks(w):
                return w.rearrange("(c p) n -> p c n", p=P)

            sp.dma_start(ctx_sb[:], chunks(ctx_t)).then_inc(k0_loaded, 16)
            sp.dma_start(wk0_sb[:], chunks(wk0)).then_inc(k0_loaded, 16)
            for dst, src in ((bk_sb, bk0), (bq_sb, bq0), (summer, sum_sel)):
                sp.dma_start(dst[:], src).then_inc(small_loaded, 16)
            sp.dma_start(bv_sb[:], bv0.partition_broadcast(P)).then_inc(small_loaded, 16)
            sp.dma_start(w_stage[:].rearrange("p (c n) -> p c n", c=KC), chunks(wq0)).then_inc(wq0_loaded, 16)
            sp.dma_start(wv0_sb[:], chunks(wv0)).then_inc(v0_loaded, 16)

            def load_x(i):
                if not upto(i, 0):
                    sp.wait_ge(x_ready, i)
                sp.dma_start(x_raw[:], at(x_t, i).rearrange("(c p) n -> p c n", p=P)).then_inc(x_loaded, 16)

            def load_mask(i):
                if not upto(i, 0):
                    sp.wait_ge(mask_ready, i)
                sp.dma_start(mask_raw[:], at(mask_t, i)).then_inc(mask_loaded, 16)

            load_x(0)
            load_mask(0)
            sp.wait_ge(wq0_ready, 1)
            sp.dma_start(sel0_raw, head_sel0).then_inc(sel_loaded, 16)
            sp.dma_start(sel1_raw, head_sel1).then_inc(sel_loaded, 16)
            sp.dma_start(beta0_b, beta0.partition_broadcast(P)).then_inc(consts_loaded, 16)
            for dst, src in ((bo0_b, bo0), (g0_b, gamma0), (bb1_b, bo1), (g1_b, gamma1), (be1_b, beta1)):
                sp.dma_start(dst[:], src.partition_broadcast(P)).then_inc(consts_loaded, 16)
            for dst, src in ((ident, identity), (g0_col, gcol0), (b0_col, bcol0)):
                sp.dma_start(dst[:], src).then_inc(consts_loaded, 16)
            load_x(1)
            load_mask(1)
            sp.wait_ge(hs_ready, 2)
            sp.wait_ge(bb1_ready, 1)
            sp.dma_start(w_stage[:].rearrange("p (c n) -> p c n", c=C0), chunks(wo0)).then_inc(wo0_loaded, 16)
            with sp.Fori(1, NB - 1) as i:
                load_x(i + 1)
                load_mask(i + 1)
            sp.wait_ge(q_psum_ready, C0 * NB)
            for dst, src in ((ctx1_sb, ctx_t), (wk1_sb, wk1), (wv1_sb, wv1)):
                sp.dma_start(dst[:], chunks(src)).then_inc(kv1_loaded, 16)

            def load_sums(i, n):
                if not upto(n, 0):
                    sp.wait_ge(den0_ready, n)
                    nc.sync.nop(nofuse=True)
                sp.dma_start(sums_in[:], at(sums_dram, i)).then_inc(sums_loaded, 16)

            def load_u(i):
                if not upto(i, 0):
                    sp.wait_ge(a0_ready, C0 * i)
                sp.dma_start(u_in[:].rearrange("p c n -> p (c n)"), at(u_dram, i)).then_inc(u_loaded, 16)

            def load_xn(i):
                if not upto(i, 0):
                    sp.wait_ge(z0_ready, QT * i)
                sp.dma_start(xn[:], at(x_n, i).rearrange("(t p) n -> p t n", p=P)).then_inc(xn_loaded, 16)

            sp.wait_ge(logits_ready, H0 * NB)
            sp.wait_ge(u_stored, 16)
            sp.wait_ge(sums_stored, 16)
            load_sums(0, 0)
            load_u(0)
            load_xn(0)
            sp.wait_ge(sums_psum_ready, NB)
            sp.dma_start(s_stage[:, 0:2048].rearrange("p (c n) -> p c n", c=KC), chunks(wq1)).then_inc(w1_loaded, 16)
            sp.dma_start(s_stage[:, 2048:4096].rearrange("p (c n) -> p c n", c=C1), chunks(wo1)).then_inc(w1_loaded, 16)
            sp.wait_ge(u_stored, 16 * NB)
            sp.wait_ge(sums_stored, 16 * NB)
            load_sums(1, 1)
            with sp.Fori(1, NB) as i:
                load_xn(i)
                load_u(i)
                load_sums((i + 1) % NB, i + 1)
            sp.wait_ge(sums_loaded, 16 * (NB + 1))
            sp.wait_ge(out_stored, 16 * NB)

        @block.tensor
        def _(pe):
            def key_product(dst, w, context, c):
                for k in range(KC):
                    last = nc.tensor.matmul(dst[:, 0:B * KEYS], w[:, k, c * P:(c + 1) * P], context[:, k, :],
                                            start=(k == 0), stop=(k == KC - 1))
                return last

            def value_product(dst, w, context, b, n):
                for k in range(KC):
                    last = nc.tensor.matmul(dst[:], context[:, k, b * KEYS:(b + 1) * KEYS],
                                            w[:, k, n * 512:(n + 1) * 512], start=(k == 0), stop=(k == KC - 1))
                return last

            pe.wait_ge(k0_loaded, 32)
            for c in range(C0):
                key_product(bank[c], wk0_sb, ctx_sb, c).then_inc(kv_psum_ready, 1)
            pe.wait_ge(v0_loaded, 16)
            for n in range(B * E0 // 512):
                pe.wait_ge(kv_done, n + 1)
                value_product(bank[n], wv0_sb, ctx_sb, n // 2, n % 2).then_inc(kv_psum_ready, 1)

            def split_product(dst, lhs, rhs, first, last):
                (lh, ll), (rh, rl) = lhs, rhs
                nc.tensor.matmul(dst, lh, rl, start=first, stop=False)
                nc.tensor.matmul(dst, ll, rh, start=False, stop=False)
                return nc.tensor.matmul(dst, lh, rh, start=False, stop=last)

            def queries0(i):
                pe.wait_ge(x_ready, i + 1)
                for c in range(C0):
                    if not (upto(i, 0) and c < 2):
                        pe.wait_ge(q_ready, C0 * i + c - 1)
                    dst = A_BANKS[c % 2]
                    for k in range(KC):
                        cols = slice(c * P, (c + 1) * P)
                        last = split_product(dst[:], (wq0_hi[:, k, cols], wq0_lo[:, k, cols]),
                                             (x_hi[:, k, :], x_lo[:, k, :]), k == 0, k == KC - 1)
                    last.then_inc(q_psum_ready, 1)

            def logits0(i, h):
                c, r = h // HC0, slice((h % HC0) * DK0, (h % HC0 + 1) * DK0)
                if h % HC0 == 0:
                    pe.wait_ge(q_ready, C0 * i + c + 1)
                if not (upto(i, 0) and h < 3):
                    pe.wait_ge(masked_ready, H0 * i + max(h - 2, 0))
                for b in range(B):
                    ks, qs = slice(b * KEYS, (b + 1) * KEYS), slice(b * QH, (b + 1) * QH)
                    last = split_product(B_BANKS[h_bank(h)][:, qs], (k0_hi[r, c, ks], k0_lo[r, c, ks]),
                                         (q0_hi[r, c, qs], q0_lo[r, c, qs]), True, True)
                last.then_inc(logits_ready, 1)

            def values0(i, j):
                pe.wait_ge(probs_ready, HG * i + j + 1)
                for c in range(2 * j, 2 * j + 2):
                    if not (upto(i, 0) and c < 2):
                        pe.wait_ge(u_saved, (C0 + 1) * i + (c - 1 if c >= 2 else c - 2))
                    for b in range(B):
                        for a in range(HC0):
                            h = HC0 * c + a
                            last = nc.tensor.matmul(U_BANKS[c % 2][a * DK0:(a + 1) * DK0, b * QH:(b + 1) * QH],
                                                    v0[:, b, h * DK0:(h + 1) * DK0],
                                                    scores[:, h, b * QH:(b + 1) * QH], start=True, stop=True)
                    last.then_inc(u_psum_ready, 1)
                if j == 0 and not upto(i, 0):
                    pe.wait_ge(u_saved, (C0 + 1) * i)
                last = row_sums(SUM_BANK, (j,))
                if j == HG - 1:
                    last.then_inc(sums_psum_ready, 1)

            def row_sums(dst, groups):
                for j in groups:
                    for g in range(G):
                        last = nc.tensor.matmul(dst[32 * g:32 * g + 32, :], summer[:, j, :],
                                                scores[:, G * j + g, :], start=(j == 0), stop=(j == HG - 1))
                return last

            def values_and_logits(i):
                for j in range(HG):
                    values0(i - 1, j)
                    for h in range(HG * j, HG * (j + 1)):
                        logits0(i, h)

            pe.wait_ge(wq0_ready, 1)
            pe.wait_ge(kv_done, C0 + B * E0 // 512)
            queries0(0)
            for h in range(H0):
                logits0(0, h)
            queries0(1)
            values_and_logits(1)
            queries0(2)
            with pe.Fori(2, NB - 1) as i:
                values_and_logits(i)
                queries0(i + 1)
            values_and_logits(NB - 1)
            pe.wait_ge(kv1_loaded, 48)
            pe.wait_ge(q_ready, C0 * NB)
            for n in range(C1 + B):
                if n >= 2:
                    pe.wait_ge(kv1_done, n - 1)
                last = (key_product(A_BANKS[n % 2], wk1_sb, ctx1_sb, n) if n < C1 else
                        value_product(A_BANKS[n % 2], wv1_sb, ctx1_sb, n - C1, 0))
                last.then_inc(kv1_psum_ready, 1)
            for j in range(HG):
                values0(NB - 1, j)

            def spread(dst, sel, r, c):
                nc.tensor.matmul(dst, sel[:, c, :], r[1][:], start=True, stop=False)
                return nc.tensor.matmul(dst, sel[:, c, :], r[0][:], start=False, stop=True)

            def spread0(i, c):
                if c >= 2:
                    pe.wait_ge(attn0_ready, C0 * i + c - 1)
                spread(R_BANKS[c % 2][:], hs0, (r0_hi, r0_lo), c).then_inc(bc0_ready, 1)

            def output0(i, c):
                pe.wait_ge(a0_ready, C0 * i + c + 1)
                if upto(i, 0):
                    pe.wait_ge(wo0_ready, c + 1)
                for n in range(QT):
                    if c == 0 and not upto(i, 1):
                        pe.wait_ge(z1_ready, QT * (i - 2) + n + 1)
                    rows = slice(n * P, (n + 1) * P)
                    last = split_product(Z_BANKS[n][:], (a_hi[:, c % 2, rows], a_lo[:, c % 2, rows]),
                                         (wo0_hi[:, c, :], wo0_lo[:, c, :]), c == 0, c == C0 - 1)
                    if c == C0 - 1 and n < QT - 1:
                        last.then_inc(o0_ready, 1)
                last.then_inc(a0_used, 1)

            def sums1_start(i):
                pe.wait_ge(scores1_ready, H1 * (i + 1) - 1)
                pe.wait_ge(probs1_ready, H1 * i + H1 // 2)
                row_sums(SUM1_BANK, range(HG // 2))

            def layer0_output(i):
                pe.wait_ge(r0_ready, i + 1)
                if upto(i, 1):
                    pe.wait_ge(kv1_done, C1 + B)
                if upto(i, 1) and i == 1:
                    pe.wait_ge(z0_ready, QT)
                for c in range(2):
                    if not upto(i, 0):
                        pe.wait_ge(scores1_ready, H1 * i - HC1 + c + 1)
                    spread0(i, c)
                if not upto(i, 0):
                    sums1_start(i - 1)
                for c in range(C0):
                    if c + 2 < C0:
                        spread0(i, c + 2)
                    output0(i, c)

            def values1(i):
                pe.wait_ge(probs1_ready, H1 * (i + 1))
                row_sums(SUM1_BANK, range(HG // 2, HG)).then_inc(sums1_psum_ready, 1)
                for c in range(C1):
                    if c in (1, 2) and not upto(i, NB - 1):
                        pe.wait_ge(attn0_ready, C0 * (i + 1) + C0 - 2 + c)
                    if c == 3:
                        pe.wait_ge(sums1_saved, i + 1)
                    for b in range(B):
                        for a in range(HC1):
                            h = HC1 * c + a
                            last = nc.tensor.matmul(PV_BANKS[c][a * DK1:(a + 1) * DK1, b * QH:(b + 1) * QH],
                                                    v1[:, b, h * DK1:(h + 1) * DK1],
                                                    scores[:, h, b * QH:(b + 1) * QH], start=True, stop=True)
                    last.then_inc(u1_psum_ready, 1)

            def spread1(i):
                pe.wait_ge(r1_ready, i + 1)
                if not upto(i, NB - 1):
                    pe.wait_ge(z0_ready, QT * (i + 2))
                for c in range(C1):
                    spread(Z_BANKS[c][:], hs1, (r1_hi, r1_lo), c).then_inc(bc1_ready, 1)

            def output1(i, c, tiles):
                if tiles[0] == 0:
                    pe.wait_ge(a1_ready, C1 * i + c + 1)
                    if c == 0:
                        pe.wait_ge(attn1_ready, C1 * (i + 1))
                for n in tiles:
                    rows = slice(n * P, (n + 1) * P)
                    last = split_product(Z_BANKS[n][:], (a_hi[:, c % 2, rows], a_lo[:, c % 2, rows]),
                                         (wo1_hi[:, c, :], wo1_lo[:, c, :]), c == 0, c == C1 - 1)
                    if n == QT - 1:
                        last.then_inc(a1_used, 1)
                    elif c == C1 - 1:
                        last.then_inc(o1_ready, 1)

            def transposes(i):
                pe.wait_ge(n0_ready, QT * (i + 1))
                if upto(i, 0):
                    pe.wait_ge(attn0_ready, C0)
                    pe.wait_ge(bq1_ready, 1)
                else:
                    pe.wait_ge(u1_saved, C1 * i)
                for c in range(KC):
                    for n in range(QT):
                        last = nc.tensor.transpose(R_BANKS[c][:, n * P:(n + 1) * P],
                                                   z0[:, n, c * P:(c + 1) * P], ident[:])
                    last.then_inc(yt_psum_ready, 1)

            def queries1(i, chunks):
                for c in chunks:
                    cols = slice(c * P, (c + 1) * P)
                    for k in range(KC):
                        if c == 0:
                            pe.wait_ge(yt_ready, KC * i + k + 1)
                        last = split_product(R_BANKS[c][:], (wq1_hi[:, k, cols], wq1_lo[:, k, cols]),
                                             (yt_hi[:, k, :], yt_lo[:, k, :]), k == 0, k == KC - 1)
                    last.then_inc(q1_psum_ready, 1)

            def logits1(i, c):
                pe.wait_ge(q1_ready, C1 * (i + 1))
                for b in range(B):
                    ks, qs = slice(b * KEYS, (b + 1) * KEYS), slice(b * QH, (b + 1) * QH)
                    for n, (kk, qq) in enumerate(((k1_hi, q1_lo), (k1_lo, q1_hi), (k1_hi, q1_hi))):
                        for g in range(HC1):
                            if b == 0 and n == 0 and c >= 1:
                                pe.wait_ge(scores1_ready, H1 * i + HC1 * (c - 1) + g + 1)
                            r = slice(g * DK1, (g + 1) * DK1)
                            last = nc.tensor.matmul(R_BANKS[g][:, qs], kk[r, c, ks], qq[r, c, qs],
                                                    start=(n == 0), stop=(n == 2))
                            if b == B - 1 and n == 2:
                                last.then_inc(logits1_ready, 1)

            def layers(i):
                layer0_output(i)
                values1(i - 1)
                transposes(i)
                queries1(i, range(C1 - 1))
                spread1(i - 1)
                queries1(i, (C1 - 1,))
                output1(i - 1, 0, (0, 1))
                for c in range(C1):
                    logits1(i, c)
                    output1(i - 1, c, (2, 3))
                    if c < C1 - 1:
                        output1(i - 1, c + 1, (0, 1))

            pe.wait_ge(u_saved, (C0 + 1) * NB)
            pe.wait_ge(consts_loaded, 16 * 9)
            layer0_output(0)
            pe.wait_ge(w1_loaded, 32)
            for c in range(C1):
                for k in range(KC):
                    last = nc.tensor.matmul(R_BANKS[3][:, c:c + 1], s_stage[:, k * E1 + c * P:k * E1 + (c + 1) * P],
                                            b0_col[:, k:k + 1], start=(k == 0), stop=(k == KC - 1))
            last.then_inc(bq1_psum_ready, 1)
            pe.wait_ge(w1_ready, 2)
            transposes(0)
            queries1(0, range(C1))
            for c in range(C1):
                logits1(0, c)
            layers(1)
            with pe.Fori(2, NB) as i:
                layers(i)
            sums1_start(NB - 1)
            values1(NB - 1)
            spread1(NB - 1)
            for c in range(C1):
                output1(NB - 1, c, range(QT))

        @block.scalar
        def _(act):
            act.wait_ge(small_loaded, 64)
            for c in range(C0):
                act.wait_ge(kv_psum_ready, c + 1)
                nc.scalar.activation(k0_hi[:, c, :], bank[c][:, 0:B * KEYS], ACT.Identity,
                                     bias=bk_sb[:, c:c + 1]).then_inc(k_hi_ready, 1)
            act.wait_ge(wq0_loaded, 16)
            nc.scalar.activation(wq0_hi[:].rearrange("p c n -> p (c n)"), w_stage[:],
                                 ACT.Copy).then_inc(wq0_hi_ready, 1)

            def x_high(i):
                act.wait_ge(x_loaded, 16 * (i + 1))
                if not upto(i, 0):
                    act.wait_ge(q_psum_ready, C0 * i)
                nc.scalar.activation(x_hi[:], x_raw[:], ACT.Copy).then_inc(x_hi_ready, 1)

            def mask_float(i):
                act.wait_ge(mask_loaded, 16 * (i + 1))
                if not upto(i, 0):
                    act.wait_ge(probs_ready, HG * i)
                nc.scalar.activation(mask_f[:], mask_raw[:], ACT.Copy).then_inc(mask_ready, 1)

            def q_high(i, c):
                act.wait_ge(q_psum_ready, C0 * i + c + 1)
                nc.scalar.activation(q0_hi[:, c, :], A_BANKS[c % 2][:], ACT.Identity,
                                     bias=bq_sb[:, c:c + 1]).then_inc(q_hi_ready, 1)

            def exponential(i, j):
                act.wait_ge(shift_ready, i + 1)
                four = scores[:, HG * j:HG * (j + 1), :]
                nc.scalar.activation(four, four, ACT.Exp, bias=neg_mx[:]).then_inc(exp_ready, 1)

            def save_u(i):
                if not upto(i, 0):
                    act.wait_ge(u_stored, 16 * i)
                    act.wait_ge(sums_stored, 16 * i)
                for c in range(C0):
                    act.wait_ge(u_psum_ready, C0 * i + c + 1)
                    nc.scalar.activation(u_out[:, c, :], U_BANKS[c % 2][:], ACT.Copy).then_inc(u_saved, 1)
                act.wait_ge(sums_psum_ready, i + 1)
                nc.scalar.activation(sums_out[:, 0:QB], SUM_BANK[:], ACT.Copy).then_inc(u_saved, 1)
                act.wait_ge(u_saved, (C0 + 1) * (i + 1))
                act.dma_start(at(u_dram, i), u_out[:].rearrange("p c n -> p (c n)")).then_inc(u_stored, 16)
                act.wait_ge(m_saved, i + 1)
                act.dma_start(at(sums_dram, i), sums_out[:]).then_inc(sums_stored, 16)

            def queries_and_exponentials(i):
                for c in range(C0):
                    q_high(i + 1, c)
                    if c < HG:
                        exponential(i, c)

            x_high(0)
            mask_float(0)
            for c in range(C0):
                q_high(0, c)
            x_high(1)
            queries_and_exponentials(0)
            act.wait_ge(sel_loaded, 32)
            nc.scalar.activation(hs0[:].rearrange("p c n -> p (c n)"), sel0_raw, ACT.Copy).then_inc(hs_ready, 1)
            nc.scalar.activation(hs1[:].rearrange("p c n -> p (c n)"), sel1_raw, ACT.Copy).then_inc(hs_ready, 1)
            mask_float(1)
            x_high(2)
            save_u(0)
            queries_and_exponentials(1)
            with act.Fori(2, NB - 1) as i:
                mask_float(i)
                x_high(i + 1)
                save_u(i - 1)
                queries_and_exponentials(i)
            mask_float(NB - 1)
            save_u(NB - 2)

            def eps_factor(i, n):
                act.wait_ge(sums_loaded, 16 * (n + 1))
                if not upto(n, 0):
                    act.wait_ge(den0_ready, n)
                nc.scalar.activation(eps_f[:], sums_in[:, QB:QB + 1], ACT.Exp, bias=m_eps[:],
                                     scale=-1.0).then_inc(eps_ready, 1)

            for j in range(HG):
                exponential(NB - 1, j)
                act.wait_ge(kv1_psum_ready, j + 1)
                nc.scalar.activation(k1_hi[:, j, :], A_BANKS[j % 2][:, 0:B * KEYS], ACT.Copy).then_inc(k1_hi_ready, 1)
            act.wait_ge(wo0_loaded, 16)
            act.wait_ge(q_psum_ready, C0 * NB)
            for c in range(2):
                nc.scalar.activation(wo0_hi[:, 4 * c:4 * c + 4, :].rearrange("p c n -> p (c n)"),
                                     w_stage[:, 2048 * c:2048 * (c + 1)], ACT.Copy).then_inc(wo0_hi_ready, 1)
            act.wait_ge(m_eps_ready, 1)
            eps_factor(0, 0)
            save_u(NB - 1)

            def a0_high(i, c):
                act.wait_ge(attn0_ready, C0 * i + c + 1)
                if c >= 2:
                    act.wait_ge(a0_used, C0 * i + c - 1)
                elif not upto(i, 1):
                    act.wait_ge(a1_used, C1 * (i - 1))
                elif upto(i, 1) and i == 1:
                    act.wait_ge(a0_used, C0)
                nc.scalar.activation(a_hi[:, c % 2, :], u_in[:, c, :], ACT.Copy).then_inc(a0_hi_ready, 1)

            def save_u1(i):
                act.wait_ge(sums1_psum_ready, i + 1)
                act.wait_ge(r0_ready, i + 2)
                nc.scalar.activation(den[:], SUM1_BANK[:], ACT.Copy).then_inc(sums1_saved, 1)
                for c in range(C1):
                    act.wait_ge(u1_psum_ready, C1 * i + c + 1)
                    if c == 0 and not upto(i, 0):
                        act.wait_ge(a1_ready, C1 * i)
                    nc.scalar.activation(u1[:, c, :], PV_BANKS[c][:], ACT.Copy).then_inc(u1_saved, 1)

            def a1_high(i, c):
                act.wait_ge(attn1_ready, C1 * i + c + 1)
                if c >= 2:
                    act.wait_ge(a1_used, C1 * i + c - 1)
                elif not upto(i, NB - 1):
                    act.wait_ge(a0_used, C0 * (i + 2))
                nc.scalar.activation(a_hi[:, c % 2, :], u1[:, c, :], ACT.Copy).then_inc(a1_hi_ready, 1)

            def yt_high(i):
                for c in range(KC):
                    act.wait_ge(yt_psum_ready, KC * i + c + 1)
                    nc.scalar.activation(yt_hi[:, c, :], R_BANKS[c][:], ACT.Copy).then_inc(yt_hi_ready, 1)

            def q1_high(i, chunks):
                for c in chunks:
                    act.wait_ge(q1_psum_ready, C1 * i + c + 1)
                    nc.scalar.activation(q1_hi[:, c, :], R_BANKS[c][:], ACT.Identity,
                                         bias=bq1_sb[:, c:c + 1]).then_inc(q1_hi_ready, 1)

            def exponential1(i, c):
                act.wait_ge(shift1_ready, C1 * i + c + 1)
                for h in range(HC1 * c, HC1 * (c + 1)):
                    nc.scalar.activation(scores[:, h, :], scores[:, h, :], ACT.Exp, bias=sh1[:, h:h + 1],
                                         scale=SCALE1).then_inc(probs1_ready, 1)

            def store_out(i):
                act.wait_ge(out_ready, QT * (i + 1))
                act.dma_start(at(out, i).rearrange("(t p) n -> p t n", p=P), z1[:]).then_inc(out_stored, 16)

            def block2(i):
                a0_high(i, 0)
                a0_high(i, 1)
                exponential1(i - 1, C1 - 1)
                for c in range(2, C0):
                    a0_high(i, c)
                if not upto(i, 1):
                    store_out(i - 2)
                save_u1(i - 1)
                yt_high(i)
                eps_factor(i + 1, i + 1)
                q1_high(i, range(C1 - 1))
                a1_high(i - 1, 0)
                a1_high(i - 1, 1)
                q1_high(i, (C1 - 1,))
                a1_high(i - 1, 2)
                exponential1(i, 0)
                a1_high(i - 1, 3)
                exponential1(i, 1)
                exponential1(i, 2)

            for c in range(C0):
                a0_high(0, c)
            act.wait_ge(w1_loaded, 32)
            for k in range(KC):
                nc.scalar.activation(wq1_hi[:, k, :], s_stage[:, k * E1:(k + 1) * E1], ACT.Copy,
                                     scale=g0_col[:, k:k + 1]).then_inc(w1_hi_ready, 1)
            nc.scalar.activation(wo1_hi[:].rearrange("p c n -> p (c n)"), s_stage[:, 2048:4096],
                                 ACT.Copy).then_inc(w1_hi_ready, 1)
            act.wait_ge(w1_ready, 2)
            act.wait_ge(bq1_ready, 1)
            yt_high(0)
            q1_high(0, range(C1))
            eps_factor(1, 1)
            for c in range(C1 - 1):
                exponential1(0, c)
            block2(1)
            with act.Fori(2, NB) as i:
                block2(i)
            exponential1(NB - 1, C1 - 1)
            store_out(NB - 2)
            save_u1(NB - 1)
            for c in range(C1):
                a1_high(NB - 1, c)
            store_out(NB - 1)

        @block.vector
        def _(dve):
            def f(ap):
                return ap.bitcast(f32)

            dve.wait_ge(small_loaded, 64)
            for c in range(C0):
                dve.wait_ge(k_hi_ready, c + 1)
                nc.vector.scalar_tensor_tensor(out=k0_lo[:, c, :], in0=bank[c][:, 0:B * KEYS],
                                               scalar=bk_sb[:, c:c + 1], in1=f(k0_hi[:, c, :]),
                                               op0=ALU.add, op1=ALU.subtract).then_inc(kv_done, 1)
            dve.wait_ge(wq0_hi_ready, 1)
            nc.vector.tensor_tensor(wq0_lo[:].rearrange("p c n -> p (c n)"), w_stage[:],
                                    f(wq0_hi[:]).rearrange("p c n -> p (c n)"), ALU.subtract).then_inc(wq0_ready, 1)
            for n in range(B * E0 // 512):
                dve.wait_ge(kv_psum_ready, C0 + n + 1)
                cols = slice((n % 2) * 512, (n % 2 + 1) * 512)
                nc.vector.tensor_tensor(v0[:, n // 2, cols], bank[n][:], bv_sb[:, cols], ALU.add).then_inc(kv_done, 1)

            def q_low(i, c):
                dve.wait_ge(q_hi_ready, C0 * i + c + 1)
                nc.vector.scalar_tensor_tensor(out=q0_lo[:, c, :], in0=A_BANKS[c % 2][:],
                                               scalar=bq_sb[:, c:c + 1], in1=f(q0_hi[:, c, :]),
                                               op0=ALU.add, op1=ALU.subtract).then_inc(q_ready, 1)

            def mask_scores(i):
                dve.wait_ge(mask_ready, i + 1)
                for h in range(H0):
                    dve.wait_ge(logits_ready, H0 * i + h + 1)
                    nc.vector.nop(nofuse=True)
                    nc.vector.tensor_tensor_reduce(out=scores[:, h, :], in0=B_BANKS[h_bank(h)][:], in1=mask_f[:],
                                                   scale=1.0, scalar=-3e38, op0=ALU.mult, op1=ALU.max,
                                                   accum_out=maxes[:, h:h + 1]).then_inc(masked_ready, 1)

            def running_max(i):
                dve.wait_ge(masked_ready, H0 * (i + 1))
                nc.vector.reduce_max(tile_mx[:], maxes[:], AX.X).then_inc(tile_max_ready, 1)
                dve.wait_ge(all_max_ready, i + 1)
                if upto(i, 0):
                    nc.vector.tensor_copy(run_max[:], all_mx[:]).then_inc(run_max_ready, 1)
                else:
                    nc.vector.tensor_tensor(run_max[:], run_max[:], all_mx[:], ALU.max).then_inc(run_max_ready, 1)
                dve.wait_ge(run_max_ready, i + 1)
                nc.vector.tensor_scalar(neg_mx[:], run_max[:], -1.0, None, ALU.mult).then_inc(shift_ready, 1)

            def save_max(i):
                if not upto(i, 0):
                    dve.wait_ge(sums_stored, 16 * i)
                nc.vector.tensor_scalar(sums_out[:, QB:SUMW], run_max[:].to_broadcast([P, SUMW - QB]),
                                        1.0, None, ALU.mult).then_inc(m_saved, 1)

            def mask_probs(i, j):
                dve.wait_ge(exp_ready, HG * i + j + 1)
                four = scores[:, HG * j:HG * (j + 1), :]
                nc.vector.tensor_tensor(four, four, mask_f[:].unsqueeze(1).to_broadcast([P, HG, QB]),
                                        ALU.mult).then_inc(probs_ready, 1)

            def block1(i):
                mask_scores(i)
                running_max(i)
                for c in range(C0):
                    q_low(i + 1, c)
                    if 1 <= c <= HG:
                        mask_probs(i, c - 1)
                save_max(i)

            for c in range(C0):
                q_low(0, c)
            block1(0)
            with dve.Fori(1, NB - 1) as i:
                block1(i)
            mask_scores(NB - 1)
            running_max(NB - 1)

            nc.vector.tensor_scalar(m_eps[:], run_max[:], math.log(SUM_EPS), None, ALU.add).then_inc(m_eps_ready, 1)
            nc.vector.memset(mhalf[:], -0.5).then_inc(mhalf_ready, 1)
            for j in range(HG):
                mask_probs(NB - 1, j)
                dve.wait_ge(k1_hi_ready, j + 1)
                nc.vector.tensor_tensor(k1_lo[:, j, :], A_BANKS[j % 2][:, 0:B * KEYS], f(k1_hi[:, j, :]),
                                        ALU.subtract).then_inc(kv1_done, 1)
            for b in range(B):
                dve.wait_ge(kv1_psum_ready, C1 + b + 1)
                nc.vector.tensor_copy(v1[:, b, :], A_BANKS[(C1 + b) % 2][:]).then_inc(kv1_done, 1)
            save_max(NB - 1)

            def reciprocals0(n, half):
                cols = slice(half * QH, (half + 1) * QH)
                if half == 0:
                    dve.wait_ge(eps_ready, n + 1)
                    nc.vector.tensor_scalar(den[:], sums_in[:, 0:QB], eps_f[:], None, ALU.add).then_inc(den0_ready, 1)
                    dve.wait_ge(den0_ready, n + 1)
                nc.vector.reciprocal(den[:, cols], den[:, cols]).then_inc(rec0_ready, 1)
                if half == 1:
                    dve.wait_ge(rec0_ready, 2 * (n + 1))
                    nc.vector.tensor_copy(r0_hi[:], den[:]).then_inc(r0_hi_ready, 1)
                    dve.wait_ge(r0_hi_ready, n + 1)
                    nc.vector.tensor_tensor(r0_lo[:], den[:], f(r0_hi[:]), ALU.subtract).then_inc(r0_ready, 1)

            for c in range(C0):
                dve.wait_ge(wo0_hi_ready, c // 4 + 1)
                nc.vector.tensor_tensor(wo0_lo[:, c, :], w_stage[:, c * D:(c + 1) * D], f(wo0_hi[:, c, :]),
                                        ALU.subtract).then_inc(wo0_ready, 1)
            reciprocals0(0, 0)
            reciprocals0(0, 1)

            def attention0(i, c):
                if c == 0:
                    dve.wait_ge(u_loaded, 16 * (i + 1))
                dve.wait_ge(bc0_ready, C0 * i + c + 1)
                nc.vector.tensor_tensor(u_in[:, c, :], u_in[:, c, :], R_BANKS[c % 2][:],
                                        ALU.mult).then_inc(attn0_ready, 1)

            def x_and_bias(i):
                dve.wait_ge(xn_loaded, 16 * (i + 1))
                nc.vector.tensor_tensor(xn[:], xn[:], bo0_b[:].unsqueeze(1).to_broadcast([P, QT, D]),
                                        ALU.add).then_inc(xb_ready, 1)

            def reciprocals1(i):
                dve.wait_ge(sums1_saved, i + 1)
                nc.vector.tensor_scalar(den[:], den[:], 1e-36, None, ALU.max).then_inc(den1_ready, 1)
                dve.wait_ge(den1_ready, i + 1)
                nc.vector.reciprocal(den[:], den[:]).then_inc(rec1_ready, 1)
                dve.wait_ge(rec1_ready, i + 1)
                nc.vector.tensor_copy(r1_hi[:], den[:]).then_inc(r1_hi_ready, 1)
                dve.wait_ge(r1_hi_ready, i + 1)
                nc.vector.tensor_tensor(r1_lo[:], den[:], f(r1_hi[:]), ALU.subtract).then_inc(r1_ready, 1)

            def attention1(i):
                dve.wait_ge(u1_saved, C1 * (i + 1))
                for c in range(C1):
                    dve.wait_ge(bc1_ready, C1 * i + c + 1)
                    nc.vector.tensor_tensor(u1[:, c, :], u1[:, c, :], Z_BANKS[c][:],
                                            ALU.mult).then_inc(attn1_ready, 1)

            def rows0(i):
                dve.wait_ge(xb_ready, i + 1)
                if not upto(i, 0):
                    dve.wait_ge(resid_ready, QT * i)
                for n in range(QT):
                    if n < QT - 1:
                        dve.wait_ge(o0_ready, (QT - 1) * i + n + 1)
                    else:
                        dve.wait_ge(a0_used, C0 * (i + 1))
                    nc.vector.tensor_tensor(z0[:, n, :], Z_BANKS[n][:], xn[:, n, :], ALU.add).then_inc(z0_ready, 1)
                    dve.wait_ge(z0_ready, QT * i + n + 1)
                    nc.vector.bn_stats(st0[:, n, :], z0[:, n, :]).then_inc(bn0_ready, 1)
                for n in range(QT):
                    dve.wait_ge(bn0_ready, QT * i + n + 1)
                    nc.vector.nop(nofuse=True)
                    nc.vector.bn_aggr(mv0[:, n, :], st0[:, n, :]).then_inc(mv0_ready, 1)

            def norm0(i):
                dve.wait_ge(rstd0_ready, i + 1)
                for n in range(QT):
                    nc.vector.tensor_scalar(z0[:, n, :], z0[:, n, :], mv0[:, n, 0:1], rs0[:, n:n + 1],
                                            ALU.subtract, ALU.mult).then_inc(n0_ready, 1)

            def yt_low(i):
                for c in range(KC):
                    dve.wait_ge(yt_hi_ready, KC * i + c + 1)
                    nc.vector.tensor_tensor(yt_lo[:, c, :], R_BANKS[c][:], f(yt_hi[:, c, :]),
                                            ALU.subtract).then_inc(yt_ready, 1)

            def q1_low(i, chunks):
                for c in chunks:
                    dve.wait_ge(q1_hi_ready, C1 * i + c + 1)
                    nc.vector.scalar_tensor_tensor(out=q1_lo[:, c, :], in0=R_BANKS[c][:], scalar=bq1_sb[:, c:c + 1],
                                                   in1=f(q1_hi[:, c, :]), op0=ALU.add,
                                                   op1=ALU.subtract).then_inc(q1_ready, 1)

            def scores_and_max1(i, c):
                for g in range(HC1):
                    h = HC1 * c + g
                    dve.wait_ge(logits1_ready, H1 * i + h + 1)
                    nc.vector.tensor_scalar(scores[:, h, :], R_BANKS[g][:], 1.0, -3e38,
                                            ALU.mult, ALU.max, accum_out=mx1[:, h:h + 1]).then_inc(scores1_ready, 1)

            def shift1(i, c):
                dve.wait_ge(amax1_ready, C1 * i + c + 1)
                hs = slice(HC1 * c, HC1 * (c + 1))
                nc.vector.tensor_scalar(sh1[:, hs], amx1[:, hs], -SCALE1, HEADROOM, ALU.mult,
                                        ALU.add).then_inc(shift1_ready, 1)

            def rows1(i):
                dve.wait_ge(resid_ready, QT * (i + 1))
                if not upto(i, 0):
                    dve.wait_ge(out_stored, 16 * i)
                for n in range(QT):
                    if n < QT - 1:
                        dve.wait_ge(o1_ready, (QT - 1) * i + n + 1)
                    else:
                        dve.wait_ge(a1_used, C1 * (i + 1))
                    nc.vector.tensor_tensor(z1[:, n, :], Z_BANKS[n][:], resid[:, n, :], ALU.add).then_inc(z1_ready, 1)

            def statistics1(i):
                for n in range(QT):
                    dve.wait_ge(z1_ready, QT * i + n + 1)
                    nc.vector.bn_stats(st1[:, n, :], z1[:, n, :]).then_inc(bn1_ready, 1)
                for n in range(QT):
                    dve.wait_ge(bn1_ready, QT * i + n + 1)
                    nc.vector.nop(nofuse=True)
                    nc.vector.bn_aggr(mv1[:, n, :], st1[:, n, :]).then_inc(mv1_ready, 1)

            def center1(i, n):
                dve.wait_ge(rstd1_ready, i + 1)
                nc.vector.scalar_tensor_tensor(out=z1[:, n, :], in0=z1[:, n, :], scalar=mv1[:, n, 0:1],
                                               in1=g1_b[:], op0=ALU.subtract, op1=ALU.mult).then_inc(ng1_ready, 1)

            def scale1(i, n):
                dve.wait_ge(ng1_ready, QT * i + n + 1)
                nc.vector.scalar_tensor_tensor(out=z1[:, n, :], in0=z1[:, n, :], scalar=rs1[:, n:n + 1],
                                               in1=be1_b[:], op0=ALU.mult, op1=ALU.add).then_inc(out_ready, 1)

            def after_output0(i):
                rows0(i)
                norm0(i)
                yt_low(i)

            def block2(i):
                norm = not upto(i, 1)
                attention0(i, 0)
                attention0(i, 1)
                shift1(i - 1, C1 - 1)
                if norm:
                    rows1(i - 2)
                    statistics1(i - 2)
                attention0(i, 2)
                x_and_bias(i)
                for c in range(3, C0):
                    attention0(i, c)
                    if norm and c < 7:
                        center1(i - 2, c - 3)
                        if c > 3:
                            scale1(i - 2, c - 4)
                if norm:
                    scale1(i - 2, QT - 1)
                after_output0(i)
                reciprocals1(i - 1)
                q1_low(i, range(C1 - 1))
                attention1(i - 1)
                q1_low(i, (C1 - 1,))
                scores_and_max1(i, 0)
                reciprocals0(i + 1, 0)
                shift1(i, 0)
                scores_and_max1(i, 1)
                reciprocals0(i + 1, 1)
                shift1(i, 1)
                scores_and_max1(i, 2)
                shift1(i, 2)
                scores_and_max1(i, 3)

            for c in range(C0):
                attention0(0, c)
            x_and_bias(0)
            for k in range(KC):
                dve.wait_ge(w1_hi_ready, k + 1)
                last = nc.vector.scalar_tensor_tensor(out=wq1_lo[:, k, :], in0=s_stage[:, k * E1:(k + 1) * E1],
                                                      scalar=g0_col[:, k:k + 1], in1=f(wq1_hi[:, k, :]),
                                                      op0=ALU.mult, op1=ALU.subtract)
            last.then_inc(w1_ready, 1)
            dve.wait_ge(w1_hi_ready, KC + 1)
            dve.wait_ge(u_stored, 16 * NB)
            dve.wait_ge(sums_stored, 16 * NB)
            nc.vector.tensor_tensor(wo1_lo[:].rearrange("p c n -> p (c n)"), s_stage[:, 2048:4096],
                                    f(wo1_hi[:]).rearrange("p c n -> p (c n)"), ALU.subtract).then_inc(w1_ready, 1)
            dve.wait_ge(bq1_psum_ready, 1)
            nc.vector.tensor_copy(bq1_sb[:], R_BANKS[3][:, 0:C1]).then_inc(bq1_ready, 1)
            after_output0(0)
            q1_low(0, range(C1))
            scores_and_max1(0, 0)
            for c in range(1, C1):
                scores_and_max1(0, c)
                shift1(0, c - 1)
            reciprocals0(1, 0)
            reciprocals0(1, 1)
            block2(1)
            with dve.Fori(2, NB) as i:
                block2(i)
            shift1(NB - 1, C1 - 1)
            rows1(NB - 2)
            statistics1(NB - 2)
            for n in range(QT):
                center1(NB - 2, n)
            for n in range(QT):
                scale1(NB - 2, n)
            reciprocals1(NB - 1)
            attention1(NB - 1)
            rows1(NB - 1)
            statistics1(NB - 1)
            for n in range(QT):
                center1(NB - 1, n)
            for n in range(QT):
                scale1(NB - 1, n)

        @block.gpsimd
        def _(pool):
            def f(ap):
                return ap.bitcast(f32)

            def x_low(i):
                pool.wait_ge(x_hi_ready, i + 1)
                nc.gpsimd.tensor_tensor(x_lo[:], x_raw[:], f(x_hi[:]), ALU.subtract).then_inc(x_ready, 1)

            def all_max(i):
                pool.wait_ge(tile_max_ready, i + 1)
                nc.gpsimd.nop(nofuse=True)
                nc.gpsimd.partition_all_reduce(all_mx[:], tile_mx[:], P, MAX).then_inc(all_max_ready, 1)

            x_low(0)
            x_low(1)
            all_max(0)
            pool.wait_ge(consts_loaded, 16 * 9)
            nc.gpsimd.tensor_tensor(bb1_b[:], bb1_b[:], beta0_b, ALU.add).then_inc(bb1_ready, 1)
            with pool.Fori(1, NB - 1) as i:
                x_low(i + 1)
                all_max(i)
            all_max(NB - 1)

            def a0_low(i, c):
                pool.wait_ge(a0_hi_ready, C0 * i + c + 1)
                nc.gpsimd.tensor_tensor(a_lo[:, c % 2, :], u_in[:, c, :], f(a_hi[:, c % 2, :]),
                                        ALU.subtract).then_inc(a0_ready, 1)

            def a1_low(i, c):
                pool.wait_ge(a1_hi_ready, C1 * i + c + 1)
                nc.gpsimd.tensor_tensor(a_lo[:, c % 2, :], u1[:, c, :], f(a_hi[:, c % 2, :]),
                                        ALU.subtract).then_inc(a1_ready, 1)

            def rstd(i, mv, rs, mv_ready, var_ready, rstd_ready):
                pool.wait_ge(mv_ready, QT * (i + 1))
                nc.gpsimd.nop(nofuse=True)
                nc.gpsimd.tensor_scalar(rs[:], mv[:, :, 1], LN_EPS, 1.0, ALU.add, ALU.mult).then_inc(var_ready, 1)
                pool.wait_ge(var_ready, i + 1)
                nc.gpsimd.tensor_tensor(rs[:], rs[:], mhalf[:], ALU.pow).then_inc(rstd_ready, 1)

            def residual1(i, c):
                n = c // 2
                if c == 0:
                    pool.wait_ge(n0_ready, QT * (i + 1))
                    if not upto(i, 0):
                        pool.wait_ge(z1_ready, QT * i)
                if c % 2 == 0:
                    nc.gpsimd.tensor_tensor(resid[:, n, :], z0[:, n, :], g0_b[:], ALU.mult).then_inc(rg_ready, 1)
                else:
                    pool.wait_ge(rg_ready, QT * i + n + 1)
                    nc.gpsimd.tensor_tensor(resid[:, n, :], resid[:, n, :], bb1_b[:], ALU.add).then_inc(resid_ready, 1)

            def head_max(i, c):
                pool.wait_ge(scores1_ready, H1 * i + HC1 * (c + 1))
                nc.gpsimd.nop(nofuse=True)
                hs = slice(HC1 * c, HC1 * (c + 1))
                nc.gpsimd.partition_all_reduce(amx1[:, hs], mx1[:, hs], P, MAX).then_inc(amax1_ready, 1)

            def block2(i):
                for c in range(C0):
                    a0_low(i, c)
                    if c == 3 and not upto(i, 1):
                        rstd(i - 2, mv1, rs1, mv1_ready, var1_ready, rstd1_ready)
                    residual1(i - 1, c)
                rstd(i, mv0, rs0, mv0_ready, var0_ready, rstd0_ready)
                a1_low(i - 1, 0)
                a1_low(i - 1, 1)
                a1_low(i - 1, 2)
                head_max(i, 0)
                a1_low(i - 1, 3)
                head_max(i, 1)
                head_max(i, 2)
                head_max(i, 3)

            for c in range(C0):
                a0_low(0, c)
            pool.wait_ge(mhalf_ready, 1)
            rstd(0, mv0, rs0, mv0_ready, var0_ready, rstd0_ready)
            for c in range(C1):
                head_max(0, c)
            block2(1)
            with pool.Fori(2, NB) as i:
                block2(i)
            for c in range(C0):
                residual1(NB - 1, c)
            rstd(NB - 2, mv1, rs1, mv1_ready, var1_ready, rstd1_ready)
            for c in range(C1):
                a1_low(NB - 1, c)
            rstd(NB - 1, mv1, rs1, mv1_ready, var1_ready, rstd1_ready)


def h_bank(h):
    return h % 3


def kernel(x, ctx_1024, mask_BxSxS2_ik1, L0_xattn_Wq, L0_xattn_bq, L0_xattn_Wk, L0_xattn_bk, L0_xattn_Wv,
           L0_xattn_bv, L0_xattn_Wo, L0_xattn_bo, L0_xattn_gamma, L0_xattn_beta, L1_xattn_Wq, L1_xattn_Wk,
           L1_xattn_Wv, L1_xattn_Wo, L1_xattn_bo, L1_xattn_ln_gamma, L1_xattn_ln_beta):
    import concourse.bacc as bacc
    from concourse.bass_utils import run_bass_kernel_spmd

    def blocks(a, last):
        return np.asarray(a).reshape(B, NB, QH, last).transpose(1, 0, 2, 3).reshape(NB, QB, last)

    xb = blocks(x, D)
    mask = blocks(mask_BxSxS2_ik1, KEYS)
    sum_sel = np.zeros((P, HG, 32), np.float32)
    for j in range(HG):
        sum_sel[:, j, j] = 1

    def head_sel(chunks, width):
        sel = np.zeros((P, chunks, P), np.float32)
        for c in range(chunks):
            for p in range(P):
                h = (c * P + p) // width
                sel[32 * (h % G) + h // G, c, p] = 1
        return sel.reshape(P, chunks * P)

    def columns(v, chunks):
        return np.asarray(v).reshape(chunks, P).T

    arrays = {
        "x_t": xb.transpose(0, 2, 1), "x_n": xb, "mask_t": mask.transpose(0, 2, 1),
        "ctx_t": np.asarray(ctx_1024).reshape(B * KEYS, D).T,
        "wq0": L0_xattn_Wq, "wk0": L0_xattn_Wk, "wv0": L0_xattn_Wv, "wo0": L0_xattn_Wo,
        "wq1": np.asarray(L1_xattn_Wq).T, "wk1": np.asarray(L1_xattn_Wk).T,
        "wv1": np.asarray(L1_xattn_Wv).T, "wo1": np.asarray(L1_xattn_Wo).T,
        "bq0": columns(L0_xattn_bq, C0), "bk0": columns(L0_xattn_bk, C0), "bv0": L0_xattn_bv,
        "bo0": L0_xattn_bo, "gamma0": L0_xattn_gamma, "beta0": L0_xattn_beta,
        "gcol0": columns(L0_xattn_gamma, KC), "bcol0": columns(L0_xattn_beta, KC),
        "bo1": L1_xattn_bo, "gamma1": L1_xattn_ln_gamma, "beta1": L1_xattn_ln_beta,
        "sum_sel": sum_sel, "head_sel0": head_sel(C0, DK0), "head_sel1": head_sel(C1, DK1),
        "identity": np.eye(P, dtype=np.float32),
    }
    arrays = {k: np.ascontiguousarray(v) for k, v in arrays.items()}
    nc = bacc.Bacc("TRN2", target_bir_lowering=False, num_devices=1, dynamic_dma_scratch_size=2048)
    args = [nc.dram_tensor(k, a.shape, mybir.dt.from_np(a.dtype), kind="ExternalInput").ap()
            for k, a in arrays.items()]
    out = nc.dram_tensor("out", (NB, QB, D), mybir.dt.float32, kind="ExternalOutput").ap()
    cross_attention_program(nc, *args, out)
    r = run_bass_kernel_spmd(nc, [arrays], core_ids=[0])
    return np.asarray(r.results[0]["out"]).reshape(NB, B, QH, D).transpose(1, 0, 2, 3).reshape(B, S, D)
```

```python
import math
from contextlib import ExitStack

import numpy as np

import concourse.bass as bass
from concourse import mybir

P = 128
B, S, D, KEYS = 2, 2048, 512, 128
H0, DK0 = 16, 64
H1, DK1 = 16, 32
E0, E1 = H0 * DK0, H1 * DK1
QB = 512
QH = QB // B
NB = B * S // QB
QT = QB // P
KC = D // P
C0, C1 = E0 // P, E1 // P
HC0, HC1 = P // DK0, P // DK1
G = 4
HG = H0 // G
LN_EPS = 1e-5
SUM_EPS = 1e-15
SCALE1 = 1.0 / math.sqrt(DK1)
HEADROOM = 40.0
SUMW = QB + 8


def cross_attention_program(nc, x_t, x_n, mask_t, ctx_t, wq0, wk0, wv0, wo0, wq1, wk1, wv1, wo1,
                            bq0, bk0, bv0, bo0, gamma0, beta0, gcol0, bcol0, bo1, gamma1, beta1,
                            sum_sel, low_row, head_sel0, head_sel1, identity, out):
    f32, f32r, i32 = mybir.dt.float32, mybir.dt.float32r, mybir.dt.int32
    ALU, ACT, AX = mybir.AluOpType, mybir.ActivationFunctionType, mybir.AxisListType
    MAX = bass.bass_isa.ReduceOp.max

    u_dram = nc.dram_tensor("u_dram", [NB, P, C0 * QB], f32, kind="Internal").ap()
    sums_dram = nc.dram_tensor("sums_dram", [NB, P, SUMW], f32, kind="Internal").ap()

    def at(dram, i):
        return dram[i] if isinstance(i, int) else dram[bass.ds(i, 1)].rearrange("a p n -> (a p) n")

    with ExitStack() as ctx:
        def sb(stack, name, shape, dt=f32):
            return stack.enter_context(nc.sbuf_tensor(name, shape, dt))

        def sem(name):
            return ctx.enter_context(nc.semaphore(name))

        def region(kib, *layouts):
            for layout in layouts:
                with ExitStack() as stack:
                    layout(stack)
            sb(ctx, f"region{len(regions)}", [P, kib * 256])
            regions.append(kib)

        regions, t = [], {}

        def put(stack, names, shape, dt=f32):
            for name in names.split():
                t[name] = sb(stack, name, shape, dt)

        def named(names):
            return (t[name] for name in names.split())

        put(ctx, "k1_hi k1_lo", [P, C1, B * KEYS], f32r)
        put(ctx, "v1", [P, B, E1])
        put(ctx, "summer", [P, HG, 32])
        put(ctx, "hs0", [P, C0, P], f32r)
        put(ctx, "hs1", [P, C1, P], f32r)
        put(ctx, "ident", [P, P])
        put(ctx, "bo0_b g0_b bb1_b g1_b be1_b", [P, D])
        put(ctx, "g0_col b0_col", [P, KC])
        put(ctx, "bq_sb bk_sb", [P, C0])
        put(ctx, "bq1_sb", [P, C1])
        put(ctx, "maxes mx1 amx1 sh1", [P, H0])
        put(ctx, "run_max tile_mx all_mx neg_mx eps_f m_eps low_rows", [P, 1])
        put(ctx, "st0 st1", [P, QT, 6])
        put(ctx, "mv0 mv1", [P, QT, 2])
        put(ctx, "rs0 rs1 mhalf", [P, QT])
        region(16, lambda k: put(k, "w_stage", [P, 4096]), lambda k: put(k, "resid z1", [P, QT, D]))
        region(32, lambda k: put(k, "yt_hi yt_lo", [P, KC, QB], f32r), lambda k: put(k, "scores", [P, H0, QB]))
        region(32, lambda k: put(k, "wq0_hi wq0_lo", [P, KC, E0], f32r),
               lambda k: put(k, "wo0_hi wo0_lo", [P, C0, D], f32r))
        region(24, lambda k: (put(k, "x_hi x_lo", [P, KC, QB], f32r), put(k, "x_raw", [P, KC, QB])),
               lambda k: (put(k, "wk1_sb wv1_sb", [P, KC, E1]), put(k, "ctx1_sb", [P, KC, B * KEYS])),
               lambda k: (put(k, "a_hi a_lo", [P, 2, QB], f32r), put(k, "q1_hi q1_lo", [P, C1, QB], f32r)))
        region(37, lambda k: (put(k, "wk0_sb wv0_sb", [P, KC, E0]), put(k, "ctx_sb", [P, KC, B * KEYS])),
               lambda k: put(k, "q0_hi q0_lo", [P, C0, QB], f32r),
               lambda k: (put(k, "u_in", [P, C0, QB]), put(k, "xn", [P, QT, D]), put(k, "sums_in", [P, SUMW]),
                          put(k, "den", [P, QB]), put(k, "r0_hi r0_split r1_hi r1_split", [P, QB], f32r)))
        region(40, lambda k: (put(k, "k0_hi k0_lo", [P, C0, B * KEYS], f32r), put(k, "v0", [P, B, E0]),
                              put(k, "u_out", [P, C0, QB])),
               lambda k: (put(k, "beside_k0_v0", [P, 24 * 256]), put(k, "bv_sb", [P, E0])),
               lambda k: (put(k, "wq1_hi wq1_lo", [P, KC, E1], f32r), put(k, "wo1_hi wo1_lo", [P, C1, D], f32r),
                          put(k, "u1", [P, C1, QB])))
        region(8, lambda k: (put(k, "mask_raw", [P, QB], i32), put(k, "mask_f", [P, QB]),
                             put(k, "sums_out", [P, SUMW])),
               lambda k: put(k, "z0", [P, QT, D]))
        k1_hi, k1_lo, v1, summer, hs0, hs1, ident = named("k1_hi k1_lo v1 summer hs0 hs1 ident")
        bo0_b, g0_b, bb1_b, g1_b, be1_b, g0_col, b0_col, bq_sb, bk_sb = named(
            "bo0_b g0_b bb1_b g1_b be1_b g0_col b0_col bq_sb bk_sb")
        bq1_sb, maxes, mx1, amx1, sh1, run_max, tile_mx, all_mx, neg_mx = named(
            "bq1_sb maxes mx1 amx1 sh1 run_max tile_mx all_mx neg_mx")
        eps_f, m_eps, low_rows, st0, st1, mv0, mv1, rs0, rs1 = named(
            "eps_f m_eps low_rows st0 st1 mv0 mv1 rs0 rs1")
        mhalf, w_stage, resid, z1, yt_hi, yt_lo, scores, wq0_hi, wq0_lo = named(
            "mhalf w_stage resid z1 yt_hi yt_lo scores wq0_hi wq0_lo")
        wo0_hi, wo0_lo, x_hi, x_lo, x_raw, wk1_sb, wv1_sb, ctx1_sb, a_hi = named(
            "wo0_hi wo0_lo x_hi x_lo x_raw wk1_sb wv1_sb ctx1_sb a_hi")
        a_lo, q1_hi, q1_lo, wk0_sb, wv0_sb, ctx_sb, q0_hi, q0_lo, u_in = named(
            "a_lo q1_hi q1_lo wk0_sb wv0_sb ctx_sb q0_hi q0_lo u_in")
        xn, sums_in, den, r0_hi, r0_split, k0_hi, k0_lo, v0, u_out = named(
            "xn sums_in den r0_hi r0_split k0_hi k0_lo v0 u_out")
        bv_sb, wq1_hi, wq1_lo, wo1_hi, wo1_lo, u1, mask_raw, mask_f, sums_out = named(
            "bv_sb wq1_hi wq1_lo wo1_hi wo1_lo u1 mask_raw mask_f sums_out")
        z0, r1_hi, r1_split = named(
            "z0 r1_hi r1_split")
        sel0_raw, sel1_raw = w_stage[:, 0:C0 * P], w_stage[:, C0 * P:(C0 + C1) * P]
        beta0_b = w_stage[:, (C0 + C1) * P:(C0 + C1) * P + D]
        s_stage = scores[:, 0:8, :].rearrange("p h n -> p (h n)")

        bank = [ctx.enter_context(nc.psum_tensor(f"bank{n}", [P, 512], f32)) for n in range(8)]
        A_BANKS, U_BANKS, SUM_BANK = bank[0:2], bank[5:7], bank[7]
        L_BANKS = [bank[0], *bank[2:5]]
        Z_BANKS, R_BANKS = bank[0:4], bank[4:8]
        PV_BANKS, SUM1_BANK = [R_BANKS[3], R_BANKS[0], R_BANKS[1], R_BANKS[2]], R_BANKS[2]

        k0_loaded, k0b_loaded, v0_loaded, wq0_loaded, kv1_loaded = (sem(n) for n in (
            "k0_loaded", "k0b_loaded", "v0_loaded", "wq0_loaded", "kv1_loaded"))
        small_loaded = sem("small_loaded")
        x_loaded, mask_loaded = sem("x_loaded"), sem("mask_loaded")
        u_stored, sums_stored = sem("u_stored"), sem("sums_stored")
        wo0_loaded, w1_loaded, consts_loaded, sel_loaded = (sem(n) for n in (
            "wo0_loaded", "w1_loaded", "consts_loaded", "sel_loaded"))
        u_loaded, sums_loaded, xn_loaded, out_stored = (sem(n) for n in (
            "u_loaded", "sums_loaded", "xn_loaded", "out_stored"))
        kv_psum_ready, k_hi_ready, kv_done, wq0_hi_ready, wq0_ready = (sem(n) for n in (
            "kv_psum_ready", "k_hi_ready", "kv_done", "wq0_hi_ready", "wq0_ready"))
        kv1_psum_ready, k1_hi_ready, kv1_done = (sem(n) for n in ("kv1_psum_ready", "k1_hi_ready", "kv1_done"))
        x_hi_ready, x_ready = sem("x_hi_ready"), sem("x_ready")
        mask_ready = sem("mask_ready")
        q_psum_ready, q_hi_ready, q_ready = sem("q_psum_ready"), sem("q_hi_ready"), sem("q_ready")
        logits_ready, masked_ready = sem("logits_ready"), sem("masked_ready")
        tile_max_ready, all_max_ready, run_max_ready, shift_ready, m_saved = (sem(n) for n in (
            "tile_max_ready", "all_max_ready", "run_max_ready", "shift_ready", "m_saved"))
        exp_ready, probs_ready = sem("exp_ready"), sem("probs_ready")
        u_psum_ready, sums_psum_ready = sem("u_psum_ready"), sem("sums_psum_ready")
        u_saved = sem("u_saved")
        m_eps_ready, mhalf_ready, wo0_hi_ready, wo0_ready, w1_hi_ready, w1_ready, hs_ready, bb1_ready = (
            sem(n) for n in ("m_eps_ready", "mhalf_ready", "wo0_hi_ready", "wo0_ready", "w1_hi_ready",
                             "w1_ready", "hs_ready", "bb1_ready"))
        bq1_psum_ready, bq1_ready = sem("bq1_psum_ready"), sem("bq1_ready")
        eps_ready, den0_ready, rec0_ready, r0_hi_ready, r0_ready = (sem(n) for n in (
            "eps_ready", "den0_ready", "rec0_ready", "r0_hi_ready", "r0_ready"))
        bc0_ready, attn0_ready, a0_hi_ready, a0_ready = (sem(n) for n in (
            "bc0_ready", "attn0_ready", "a0_hi_ready", "a0_ready"))
        a0_used, a1_used = sem("a0_used"), sem("a1_used")
        o0_ready, o1_ready = sem("o0_ready"), sem("o1_ready")
        xb_ready = sem("xb_ready")
        z0_ready, bn0_ready, mv0_ready, n0_ready = (sem(n) for n in (
            "z0_ready", "bn0_ready", "mv0_ready", "n0_ready"))
        var0_ready, rstd0_ready = sem("var0_ready"), sem("rstd0_ready")
        rg_ready, resid_ready = sem("rg_ready"), sem("resid_ready")
        yt_psum_ready, yt_hi_ready, yt_ready = (sem(n) for n in (
            "yt_psum_ready", "yt_hi_ready", "yt_ready"))
        q1_psum_ready, q1_hi_ready, q1_ready = (sem(n) for n in (
            "q1_psum_ready", "q1_hi_ready", "q1_ready"))
        logits1_ready, scores1_ready = sem("logits1_ready"), sem("scores1_ready")
        amax1_ready, shift1_ready = sem("amax1_ready"), sem("shift1_ready")
        probs1_ready = sem("probs1_ready")
        sums1_psum_ready, sums1_saved, den1_ready, rec1_ready, r1_hi_ready, r1_ready = (sem(n) for n in (
            "sums1_psum_ready", "sums1_saved", "den1_ready", "rec1_ready", "r1_hi_ready", "r1_ready"))
        u1_psum_ready, u1_saved, bc1_ready, attn1_ready, a1_hi_ready, a1_ready = (sem(n) for n in (
            "u1_psum_ready", "u1_saved", "bc1_ready", "attn1_ready", "a1_hi_ready", "a1_ready"))
        z1_ready, bn1_ready, mv1_ready, ng1_ready, out_ready = (sem(n) for n in (
            "z1_ready", "bn1_ready", "mv1_ready", "ng1_ready", "out_ready"))
        var1_ready, rstd1_ready = sem("var1_ready"), sem("rstd1_ready")

        block = ctx.enter_context(nc.Block())

        def upto(i, n):
            return isinstance(i, int) and i <= n

        @block.sync
        def _(sp):
            def chunks(w):
                return w.rearrange("(c p) n -> p c n", p=P)

            sp.dma_start(ctx_sb[:], chunks(ctx_t)).then_inc(k0_loaded, 16)
            sp.dma_start(wk0_sb[:, :, 0:E0 // 2], chunks(wk0)[:, :, 0:E0 // 2]).then_inc(k0_loaded, 16)
            sp.dma_start(wk0_sb[:, :, E0 // 2:E0], chunks(wk0)[:, :, E0 // 2:E0]).then_inc(k0b_loaded, 16)
            for dst, src in ((bk_sb, bk0), (bq_sb, bq0), (summer, sum_sel), (low_rows, low_row)):
                sp.dma_start(dst[:], src).then_inc(small_loaded, 16)
            sp.dma_start(bv_sb[:], bv0.partition_broadcast(P)).then_inc(small_loaded, 16)
            sp.dma_start(w_stage[:].rearrange("p (c n) -> p c n", c=KC), chunks(wq0)).then_inc(wq0_loaded, 16)
            sp.dma_start(wv0_sb[:], chunks(wv0)).then_inc(v0_loaded, 16)

            def load_x(i):
                if not upto(i, 0):
                    sp.wait_ge(x_ready, i)
                sp.dma_start(x_raw[:], at(x_t, i).rearrange("(c p) n -> p c n", p=P)).then_inc(x_loaded, 16)

            def load_mask(i):
                if not upto(i, 0):
                    sp.wait_ge(mask_ready, i)
                sp.dma_start(mask_raw[:], at(mask_t, i)).then_inc(mask_loaded, 16)

            load_x(0)
            load_mask(0)
            sp.wait_ge(wq0_ready, 1)
            sp.dma_start(sel0_raw, head_sel0).then_inc(sel_loaded, 16)
            sp.dma_start(sel1_raw, head_sel1).then_inc(sel_loaded, 16)
            sp.dma_start(beta0_b, beta0.partition_broadcast(P)).then_inc(consts_loaded, 16)
            for dst, src in ((bo0_b, bo0), (g0_b, gamma0), (bb1_b, bo1), (g1_b, gamma1), (be1_b, beta1)):
                sp.dma_start(dst[:], src.partition_broadcast(P)).then_inc(consts_loaded, 16)
            for dst, src in ((ident, identity), (g0_col, gcol0), (b0_col, bcol0)):
                sp.dma_start(dst[:], src).then_inc(consts_loaded, 16)
            load_x(1)
            load_mask(1)
            load_x(2)
            load_mask(2)
            sp.wait_ge(hs_ready, 2)
            sp.wait_ge(bb1_ready, 1)
            sp.dma_start(w_stage[:].rearrange("p (c n) -> p c n", c=C0), chunks(wo0)).then_inc(wo0_loaded, 16)
            with sp.Fori(2, NB - 1) as i:
                load_x(i + 1)
                load_mask(i + 1)
            sp.wait_ge(q_psum_ready, C0 * NB)
            for dst, src in ((ctx1_sb, ctx_t), (wk1_sb, wk1), (wv1_sb, wv1)):
                sp.dma_start(dst[:], chunks(src)).then_inc(kv1_loaded, 16)

            def load_sums(i, n):
                if not upto(n, 0):
                    sp.wait_ge(den0_ready, n)
                    nc.sync.nop(nofuse=True)
                sp.dma_start(sums_in[:], at(sums_dram, i)).then_inc(sums_loaded, 16)

            def load_u(i):
                if not upto(i, 0):
                    sp.wait_ge(a0_ready, C0 * i)
                sp.dma_start(u_in[:].rearrange("p c n -> p (c n)"), at(u_dram, i)).then_inc(u_loaded, 16)

            def load_xn(i):
                if not upto(i, 0):
                    sp.wait_ge(z0_ready, QT * i)
                sp.dma_start(xn[:], at(x_n, i).rearrange("(t p) n -> p t n", p=P)).then_inc(xn_loaded, 16)

            sp.wait_ge(logits_ready, H0 * NB)
            sp.wait_ge(u_stored, 16)
            sp.wait_ge(sums_stored, 16)
            load_sums(0, 0)
            load_u(0)
            load_xn(0)
            sp.wait_ge(sums_psum_ready, NB)
            sp.dma_start(s_stage[:, 0:2048].rearrange("p (c n) -> p c n", c=KC), chunks(wq1)).then_inc(w1_loaded, 16)
            sp.dma_start(s_stage[:, 2048:4096].rearrange("p (c n) -> p c n", c=C1), chunks(wo1)).then_inc(w1_loaded, 16)
            sp.wait_ge(u_stored, 16 * NB)
            sp.wait_ge(sums_stored, 16 * NB)
            load_sums(1, 1)
            with sp.Fori(1, NB) as i:
                load_xn(i)
                load_u(i)
                load_sums((i + 1) % NB, i + 1)
            sp.wait_ge(sums_loaded, 16 * (NB + 1))
            sp.wait_ge(out_stored, 16 * (NB + 1))

        @block.tensor
        def _(pe):
            def key_product(dst, w, context, c):
                for k in range(KC):
                    last = nc.tensor.matmul(dst[:, 0:B * KEYS], w[:, k, c * P:(c + 1) * P], context[:, k, :],
                                            start=(k == 0), stop=(k == KC - 1))
                return last

            def value_product(dst, w, context, b, n):
                for k in range(KC):
                    last = nc.tensor.matmul(dst[:], context[:, k, b * KEYS:(b + 1) * KEYS],
                                            w[:, k, n * 512:(n + 1) * 512], start=(k == 0), stop=(k == KC - 1))
                return last

            pe.wait_ge(k0_loaded, 32)
            for c in range(C0):
                if c == C0 // 2:
                    pe.wait_ge(k0b_loaded, 16)
                key_product(bank[c], wk0_sb, ctx_sb, c).then_inc(kv_psum_ready, 1)
            pe.wait_ge(v0_loaded, 16)
            for n in range(B * E0 // 512):
                pe.wait_ge(kv_done, n + 1)
                value_product(bank[n], wv0_sb, ctx_sb, n // 2, n % 2).then_inc(kv_psum_ready, 1)

            def split_product(dst, lhs, rhs, first, last):
                (lh, ll), (rh, rl) = lhs, rhs
                nc.tensor.matmul(dst, lh, rl, start=first, stop=False)
                nc.tensor.matmul(dst, ll, rh, start=False, stop=False)
                return nc.tensor.matmul(dst, lh, rh, start=False, stop=last)

            def queries0(i):
                pe.wait_ge(x_ready, i + 1)
                for c in range(C0):
                    if not (upto(i, 0) and c < 2):
                        pe.wait_ge(q_ready, C0 * i + c - 1)
                    if c == 0 and not upto(i, 0):
                        pe.wait_ge(masked_ready, H0 * i - HC0)
                    dst = A_BANKS[c % 2]
                    for k in range(KC):
                        cols = slice(c * P, (c + 1) * P)
                        last = split_product(dst[:], (wq0_hi[:, k, cols], wq0_lo[:, k, cols]),
                                             (x_hi[:, k, :], x_lo[:, k, :]), k == 0, k == KC - 1)
                    last.then_inc(q_psum_ready, 1)

            def logits0(i, c):
                pe.wait_ge(q_ready, C0 * i + max(c + 1, C0 - 1))
                if not (upto(i, 0) and c < 2):
                    pe.wait_ge(masked_ready, H0 * i + HC0 * (c - 1))
                for b in range(B):
                    ks, qs = slice(b * KEYS, (b + 1) * KEYS), slice(b * QH, (b + 1) * QH)
                    for n, (kk, qq) in enumerate(((k0_hi, q0_lo), (k0_lo, q0_hi), (k0_hi, q0_hi))):
                        for a in range(HC0):
                            r = slice(a * DK0, (a + 1) * DK0)
                            last = nc.tensor.matmul(L_BANKS[(HC0 * c + a) % 4][:, qs], kk[r, c, ks], qq[r, c, qs],
                                                    start=(n == 0), stop=(n == 2))
                            if b == B - 1 and n == 2:
                                last.then_inc(logits_ready, 1)

            def values0(i, j):
                pe.wait_ge(probs_ready, HG * i + j + 1)
                for c in range(2 * j, 2 * j + 2):
                    if not (upto(i, 0) and c < 2):
                        pe.wait_ge(u_saved, (C0 + 1) * i + (c - 1 if c >= 2 else c - 2))
                    for b in range(B):
                        for a in range(HC0):
                            h = HC0 * c + a
                            last = nc.tensor.matmul(U_BANKS[c % 2][a * DK0:(a + 1) * DK0, b * QH:(b + 1) * QH],
                                                    v0[:, b, h * DK0:(h + 1) * DK0],
                                                    scores[:, h, b * QH:(b + 1) * QH], start=True, stop=True)
                    last.then_inc(u_psum_ready, 1)
                if j == 0 and not upto(i, 0):
                    pe.wait_ge(u_saved, (C0 + 1) * i)
                last = row_sums(SUM_BANK, (j,))
                if j == HG - 1:
                    last.then_inc(sums_psum_ready, 1)

            def row_sums(dst, groups):
                for j in groups:
                    for g in range(G):
                        last = nc.tensor.matmul(dst[32 * g:32 * g + 32, :], summer[:, j, :],
                                                scores[:, G * j + g, :], start=(j == 0), stop=(j == HG - 1))
                return last

            def values_and_logits(i):
                for j in range(HG):
                    values0(i - 1, j)
                    for c in range(2 * j, 2 * j + 2):
                        logits0(i, c)

            pe.wait_ge(wq0_ready, 1)
            pe.wait_ge(kv_done, C0 + B * E0 // 512)
            queries0(0)
            for c in range(C0):
                logits0(0, c)
            queries0(1)
            values_and_logits(1)
            queries0(2)
            with pe.Fori(2, NB - 1) as i:
                values_and_logits(i)
                queries0(i + 1)
            values_and_logits(NB - 1)
            pe.wait_ge(kv1_loaded, 48)
            pe.wait_ge(q_ready, C0 * NB)
            pe.wait_ge(masked_ready, H0 * NB - HC0)
            for n in range(C1 + B):
                if n >= 2:
                    pe.wait_ge(kv1_done, n - 1)
                last = (key_product(A_BANKS[n % 2], wk1_sb, ctx1_sb, n) if n < C1 else
                        value_product(A_BANKS[n % 2], wv1_sb, ctx1_sb, n - C1, 0))
                last.then_inc(kv1_psum_ready, 1)
            for j in range(HG):
                values0(NB - 1, j)

            def spread(dst, sel, r, c):
                return nc.tensor.matmul(dst, sel[:, c, :], r[:], start=True, stop=True)

            def spread0(i, c):
                if c >= 2:
                    pe.wait_ge(attn0_ready, C0 * i + c - 1)
                spread(R_BANKS[c % 2][:], hs0, r0_split, c).then_inc(bc0_ready, 1)

            def output0(i, c):
                pe.wait_ge(a0_ready, C0 * i + c + 1)
                if upto(i, 0):
                    pe.wait_ge(wo0_ready, c + 1)
                for n in range(QT):
                    if c == 0 and not upto(i, 1):
                        pe.wait_ge(z1_ready, QT * (i - 2) + n + 1)
                    rows = slice(n * P, (n + 1) * P)
                    last = split_product(Z_BANKS[n][:], (a_hi[:, c % 2, rows], a_lo[:, c % 2, rows]),
                                         (wo0_hi[:, c, :], wo0_lo[:, c, :]), c == 0, c == C0 - 1)
                    if c == C0 - 1 and n < QT - 1:
                        last.then_inc(o0_ready, 1)
                last.then_inc(a0_used, 1)

            def sums1_start(i):
                pe.wait_ge(scores1_ready, H1 * (i + 1) - 1)
                pe.wait_ge(probs1_ready, H1 * i + H1 // 2)
                row_sums(SUM1_BANK, range(HG // 2))

            def layer0_output(i):
                pe.wait_ge(r0_ready, i + 1)
                if upto(i, 0):
                    pe.wait_ge(kv1_done, C1 + B)
                if upto(i, 1) and not upto(i, 0):
                    pe.wait_ge(z0_ready, QT)
                for c in range(2):
                    if not upto(i, 0):
                        pe.wait_ge(scores1_ready, H1 * i - HC1 + c + 1)
                    spread0(i, c)
                if not upto(i, 0):
                    sums1_start(i - 1)
                for c in range(C0):
                    if c + 2 < C0:
                        spread0(i, c + 2)
                    output0(i, c)

            def values1(i):
                pe.wait_ge(probs1_ready, H1 * (i + 1))
                row_sums(SUM1_BANK, range(HG // 2, HG)).then_inc(sums1_psum_ready, 1)
                for c in range(C1):
                    if c in (1, 2) and not upto(i, NB - 1):
                        pe.wait_ge(attn0_ready, C0 * (i + 1) + C0 - 2 + c)
                    if c == 3:
                        pe.wait_ge(sums1_saved, i + 1)
                    for b in range(B):
                        for a in range(HC1):
                            h = HC1 * c + a
                            last = nc.tensor.matmul(PV_BANKS[c][a * DK1:(a + 1) * DK1, b * QH:(b + 1) * QH],
                                                    v1[:, b, h * DK1:(h + 1) * DK1],
                                                    scores[:, h, b * QH:(b + 1) * QH], start=True, stop=True)
                    last.then_inc(u1_psum_ready, 1)

            def spread1(i):
                pe.wait_ge(r1_ready, i + 1)
                if not upto(i, NB - 1):
                    pe.wait_ge(z0_ready, QT * (i + 2))
                for c in range(C1):
                    spread(Z_BANKS[c][:], hs1, r1_split, c).then_inc(bc1_ready, 1)

            def output1(i, c, tiles):
                if tiles[0] == 0:
                    pe.wait_ge(a1_ready, C1 * i + c + 1)
                    if c == 0:
                        pe.wait_ge(attn1_ready, C1 * (i + 1))
                for n in tiles:
                    rows = slice(n * P, (n + 1) * P)
                    last = split_product(Z_BANKS[n][:], (a_hi[:, c % 2, rows], a_lo[:, c % 2, rows]),
                                         (wo1_hi[:, c, :], wo1_lo[:, c, :]), c == 0, c == C1 - 1)
                    if n == QT - 1:
                        last.then_inc(a1_used, 1)
                    elif c == C1 - 1:
                        last.then_inc(o1_ready, 1)

            def transposes(i):
                pe.wait_ge(n0_ready, QT * (i + 1))
                if upto(i, 0):
                    pe.wait_ge(attn0_ready, C0)
                    pe.wait_ge(bq1_ready, 1)
                else:
                    pe.wait_ge(u1_saved, C1 * i)
                for c in range(KC):
                    for n in range(QT):
                        last = nc.tensor.transpose(R_BANKS[c][:, n * P:(n + 1) * P],
                                                   z0[:, n, c * P:(c + 1) * P], ident[:])
                    last.then_inc(yt_psum_ready, 1)

            def queries1(i, chunks):
                for c in chunks:
                    cols = slice(c * P, (c + 1) * P)
                    for k in range(KC):
                        if c == 0:
                            pe.wait_ge(yt_ready, KC * i + k + 1)
                        last = split_product(R_BANKS[c][:], (wq1_hi[:, k, cols], wq1_lo[:, k, cols]),
                                             (yt_hi[:, k, :], yt_lo[:, k, :]), k == 0, k == KC - 1)
                    last.then_inc(q1_psum_ready, 1)

            def logits1(i, c):
                pe.wait_ge(q1_ready, C1 * (i + 1))
                for b in range(B):
                    ks, qs = slice(b * KEYS, (b + 1) * KEYS), slice(b * QH, (b + 1) * QH)
                    for n, (kk, qq) in enumerate(((k1_hi, q1_lo), (k1_lo, q1_hi), (k1_hi, q1_hi))):
                        for g in range(HC1):
                            if b == 0 and n == 0 and c >= 1:
                                pe.wait_ge(scores1_ready, H1 * i + HC1 * (c - 1) + g + 1)
                            r = slice(g * DK1, (g + 1) * DK1)
                            last = nc.tensor.matmul(R_BANKS[g][:, qs], kk[r, c, ks], qq[r, c, qs],
                                                    start=(n == 0), stop=(n == 2))
                            if b == B - 1 and n == 2:
                                last.then_inc(logits1_ready, 1)

            def layers(i):
                layer0_output(i)
                values1(i - 1)
                transposes(i)
                queries1(i, range(C1 - 1))
                spread1(i - 1)
                queries1(i, (C1 - 1,))
                output1(i - 1, 0, (0, 1))
                for c in range(C1):
                    logits1(i, c)
                    output1(i - 1, c, (2, 3))
                    if c < C1 - 1:
                        output1(i - 1, c + 1, (0, 1))

            pe.wait_ge(u_saved, (C0 + 1) * NB)
            pe.wait_ge(consts_loaded, 16 * 9)
            layer0_output(0)
            pe.wait_ge(w1_loaded, 32)
            for c in range(C1):
                for k in range(KC):
                    last = nc.tensor.matmul(R_BANKS[3][:, c:c + 1], s_stage[:, k * E1 + c * P:k * E1 + (c + 1) * P],
                                            b0_col[:, k:k + 1], start=(k == 0), stop=(k == KC - 1))
            last.then_inc(bq1_psum_ready, 1)
            pe.wait_ge(w1_ready, 2)
            transposes(0)
            queries1(0, range(C1))
            for c in range(C1):
                logits1(0, c)
            layers(1)
            with pe.Fori(2, NB) as i:
                layers(i)
            sums1_start(NB - 1)
            values1(NB - 1)
            spread1(NB - 1)
            for c in range(C1 - 2):
                output1(NB - 1, c, range(QT))
            for n in range(QT):
                output1(NB - 1, C1 - 2, (n,))
                output1(NB - 1, C1 - 1, (n,))

        @block.scalar
        def _(act):
            act.wait_ge(small_loaded, 80)
            for c in range(C0):
                act.wait_ge(kv_psum_ready, c + 1)
                nc.scalar.activation(k0_hi[:, c, :], bank[c][:, 0:B * KEYS], ACT.Identity,
                                     bias=bk_sb[:, c:c + 1]).then_inc(k_hi_ready, 1)
            act.wait_ge(wq0_loaded, 16)
            nc.scalar.activation(wq0_hi[:].rearrange("p c n -> p (c n)"), w_stage[:],
                                 ACT.Copy).then_inc(wq0_hi_ready, 1)

            def x_high(i):
                act.wait_ge(x_loaded, 16 * (i + 1))
                if not upto(i, 0):
                    act.wait_ge(q_psum_ready, C0 * i)
                nc.scalar.activation(x_hi[:], x_raw[:], ACT.Copy).then_inc(x_hi_ready, 1)

            def mask_float(i):
                act.wait_ge(mask_loaded, 16 * (i + 1))
                if not upto(i, 0):
                    act.wait_ge(probs_ready, HG * i)
                nc.scalar.activation(mask_f[:], mask_raw[:], ACT.Copy).then_inc(mask_ready, 1)

            def q_high(i, c):
                act.wait_ge(q_psum_ready, C0 * i + c + 1)
                nc.scalar.activation(q0_hi[:, c, :], A_BANKS[c % 2][:], ACT.Identity,
                                     bias=bq_sb[:, c:c + 1]).then_inc(q_hi_ready, 1)

            def exponential(i, j):
                act.wait_ge(shift_ready, i + 1)
                four = scores[:, HG * j:HG * (j + 1), :]
                nc.scalar.activation(four, four, ACT.Exp, bias=neg_mx[:]).then_inc(exp_ready, 1)

            def save_u(i):
                if not upto(i, 0):
                    act.wait_ge(u_stored, 16 * i)
                    act.wait_ge(sums_stored, 16 * i)
                for c in range(C0):
                    act.wait_ge(u_psum_ready, C0 * i + c + 1)
                    nc.scalar.activation(u_out[:, c, :], U_BANKS[c % 2][:], ACT.Copy).then_inc(u_saved, 1)
                act.wait_ge(sums_psum_ready, i + 1)
                nc.scalar.activation(sums_out[:, 0:QB], SUM_BANK[:], ACT.Copy).then_inc(u_saved, 1)
                act.wait_ge(u_saved, (C0 + 1) * (i + 1))
                act.dma_start(at(u_dram, i), u_out[:].rearrange("p c n -> p (c n)")).then_inc(u_stored, 16)
                act.wait_ge(m_saved, i + 1)
                act.dma_start(at(sums_dram, i), sums_out[:]).then_inc(sums_stored, 16)

            def queries_and_exponentials(i):
                for c in range(C0):
                    q_high(i + 1, c)
                    if c < HG:
                        exponential(i, c)

            x_high(0)
            mask_float(0)
            for c in range(C0):
                q_high(0, c)
            x_high(1)
            queries_and_exponentials(0)
            act.wait_ge(sel_loaded, 32)
            nc.scalar.activation(hs0[:].rearrange("p c n -> p (c n)"), sel0_raw, ACT.Copy).then_inc(hs_ready, 1)
            nc.scalar.activation(hs1[:].rearrange("p c n -> p (c n)"), sel1_raw, ACT.Copy).then_inc(hs_ready, 1)
            mask_float(1)
            x_high(2)
            save_u(0)
            queries_and_exponentials(1)
            with act.Fori(2, NB - 1) as i:
                mask_float(i)
                x_high(i + 1)
                save_u(i - 1)
                queries_and_exponentials(i)
            mask_float(NB - 1)
            save_u(NB - 2)

            def eps_factor(i, n):
                act.wait_ge(sums_loaded, 16 * (n + 1))
                if not upto(n, 0):
                    act.wait_ge(den0_ready, n)
                nc.scalar.activation(eps_f[:], sums_in[:, QB:QB + 1], ACT.Exp, bias=m_eps[:],
                                     scale=-1.0).then_inc(eps_ready, 1)

            for j in range(HG):
                exponential(NB - 1, j)
                act.wait_ge(kv1_psum_ready, j + 1)
                nc.scalar.activation(k1_hi[:, j, :], A_BANKS[j % 2][:, 0:B * KEYS], ACT.Copy).then_inc(k1_hi_ready, 1)
            act.wait_ge(wo0_loaded, 16)
            act.wait_ge(q_psum_ready, C0 * NB)
            for c in range(2):
                nc.scalar.activation(wo0_hi[:, 4 * c:4 * c + 4, :].rearrange("p c n -> p (c n)"),
                                     w_stage[:, 2048 * c:2048 * (c + 1)], ACT.Copy).then_inc(wo0_hi_ready, 1)
            act.wait_ge(m_eps_ready, 1)
            eps_factor(0, 0)
            save_u(NB - 1)

            def a0_high(i, c):
                act.wait_ge(attn0_ready, C0 * i + c + 1)
                if c >= 2:
                    act.wait_ge(a0_used, C0 * i + c - 1)
                elif not upto(i, 1):
                    act.wait_ge(a1_used, C1 * (i - 1))
                elif not upto(i, 0):
                    act.wait_ge(a0_used, C0)
                nc.scalar.activation(a_hi[:, c % 2, :], u_in[:, c, :], ACT.Copy).then_inc(a0_hi_ready, 1)

            def save_u1(i):
                act.wait_ge(sums1_psum_ready, i + 1)
                act.wait_ge(r0_ready, i + 2)
                nc.scalar.activation(den[:], SUM1_BANK[:], ACT.Copy).then_inc(sums1_saved, 1)
                for c in range(C1):
                    act.wait_ge(u1_psum_ready, C1 * i + c + 1)
                    if c == 0 and not upto(i, 0):
                        act.wait_ge(a1_ready, C1 * i)
                    nc.scalar.activation(u1[:, c, :], PV_BANKS[c][:], ACT.Copy).then_inc(u1_saved, 1)

            def a1_high(i, c):
                act.wait_ge(attn1_ready, C1 * i + c + 1)
                if c >= 2:
                    act.wait_ge(a1_used, C1 * i + c - 1)
                elif not upto(i, NB - 1):
                    act.wait_ge(a0_used, C0 * (i + 2))
                nc.scalar.activation(a_hi[:, c % 2, :], u1[:, c, :], ACT.Copy).then_inc(a1_hi_ready, 1)

            def yt_high(i):
                for c in range(KC):
                    act.wait_ge(yt_psum_ready, KC * i + c + 1)
                    nc.scalar.activation(yt_hi[:, c, :], R_BANKS[c][:], ACT.Copy).then_inc(yt_hi_ready, 1)

            def q1_high(i, chunks):
                for c in chunks:
                    act.wait_ge(q1_psum_ready, C1 * i + c + 1)
                    nc.scalar.activation(q1_hi[:, c, :], R_BANKS[c][:], ACT.Identity,
                                         bias=bq1_sb[:, c:c + 1]).then_inc(q1_hi_ready, 1)

            def exponential1(i, c):
                act.wait_ge(shift1_ready, C1 * i + c + 1)
                for h in range(HC1 * c, HC1 * (c + 1)):
                    nc.scalar.activation(scores[:, h, :], scores[:, h, :], ACT.Exp, bias=sh1[:, h:h + 1],
                                         scale=SCALE1).then_inc(probs1_ready, 1)

            def store_out(i):
                act.wait_ge(out_ready, QT * (i + 1))
                act.dma_start(at(out, i).rearrange("(t p) n -> p t n", p=P), z1[:]).then_inc(out_stored, 16)

            def block2(i):
                a0_high(i, 0)
                a0_high(i, 1)
                a0_high(i, 2)
                exponential1(i - 1, C1 - 1)
                for c in range(3, C0):
                    a0_high(i, c)
                if not upto(i, 1):
                    store_out(i - 2)
                save_u1(i - 1)
                yt_high(i)
                eps_factor(i + 1, i + 1)
                q1_high(i, range(C1 - 1))
                a1_high(i - 1, 0)
                a1_high(i - 1, 1)
                q1_high(i, (C1 - 1,))
                a1_high(i - 1, 2)
                exponential1(i, 0)
                a1_high(i - 1, 3)
                exponential1(i, 1)
                exponential1(i, 2)

            for c in range(C0):
                a0_high(0, c)
            act.wait_ge(w1_loaded, 32)
            for k in range(KC):
                nc.scalar.activation(wq1_hi[:, k, :], s_stage[:, k * E1:(k + 1) * E1], ACT.Copy,
                                     scale=g0_col[:, k:k + 1]).then_inc(w1_hi_ready, 1)
            nc.scalar.activation(wo1_hi[:].rearrange("p c n -> p (c n)"), s_stage[:, 2048:4096],
                                 ACT.Copy).then_inc(w1_hi_ready, 1)
            act.wait_ge(w1_ready, 2)
            act.wait_ge(bq1_ready, 1)
            yt_high(0)
            q1_high(0, range(C1))
            eps_factor(1, 1)
            for c in range(C1 - 1):
                exponential1(0, c)
            block2(1)
            with act.Fori(2, NB) as i:
                block2(i)
            exponential1(NB - 1, C1 - 1)
            save_u1(NB - 1)
            a1_high(NB - 1, 0)
            a1_high(NB - 1, 1)
            store_out(NB - 2)
            a1_high(NB - 1, 2)
            a1_high(NB - 1, 3)
            for half in range(2):
                act.wait_ge(out_ready, QT * (NB - 1) + 2 * half + 2)
                act.dma_start(out[NB - 1].rearrange("(t p) n -> p t n", p=P)[:, 2 * half:2 * half + 2, :],
                              z1[:, 2 * half:2 * half + 2, :]).then_inc(out_stored, 16)

        @block.vector
        def _(dve):
            def f(ap):
                return ap.bitcast(f32)

            dve.wait_ge(small_loaded, 80)
            for c in range(C0):
                dve.wait_ge(k_hi_ready, c + 1)
                nc.vector.scalar_tensor_tensor(out=k0_lo[:, c, :], in0=bank[c][:, 0:B * KEYS],
                                               scalar=bk_sb[:, c:c + 1], in1=f(k0_hi[:, c, :]),
                                               op0=ALU.add, op1=ALU.subtract).then_inc(kv_done, 1)
            dve.wait_ge(wq0_hi_ready, 1)
            nc.vector.tensor_tensor(wq0_lo[:].rearrange("p c n -> p (c n)"), w_stage[:],
                                    f(wq0_hi[:]).rearrange("p c n -> p (c n)"), ALU.subtract).then_inc(wq0_ready, 1)
            for n in range(B * E0 // 512):
                dve.wait_ge(kv_psum_ready, C0 + n + 1)
                cols = slice((n % 2) * 512, (n % 2 + 1) * 512)
                nc.vector.tensor_tensor(v0[:, n // 2, cols], bank[n][:], bv_sb[:, cols], ALU.add).then_inc(kv_done, 1)

            def q_low(i, c):
                dve.wait_ge(q_hi_ready, C0 * i + c + 1)
                nc.vector.scalar_tensor_tensor(out=q0_lo[:, c, :], in0=A_BANKS[c % 2][:],
                                               scalar=bq_sb[:, c:c + 1], in1=f(q0_hi[:, c, :]),
                                               op0=ALU.add, op1=ALU.subtract).then_inc(q_ready, 1)

            def mask_scores(i):
                dve.wait_ge(mask_ready, i + 1)
                for h in range(H0):
                    dve.wait_ge(logits_ready, H0 * i + h + 1)
                    nc.vector.nop(nofuse=True)
                    nc.vector.tensor_tensor_reduce(out=scores[:, h, :], in0=L_BANKS[h % 4][:], in1=mask_f[:],
                                                   scale=1.0, scalar=-3e38, op0=ALU.mult, op1=ALU.max,
                                                   accum_out=maxes[:, h:h + 1]).then_inc(masked_ready, 1)

            def running_max(i):
                dve.wait_ge(masked_ready, H0 * (i + 1))
                nc.vector.reduce_max(tile_mx[:], maxes[:], AX.X).then_inc(tile_max_ready, 1)
                dve.wait_ge(all_max_ready, i + 1)
                if upto(i, 0):
                    nc.vector.tensor_copy(run_max[:], all_mx[:]).then_inc(run_max_ready, 1)
                else:
                    nc.vector.tensor_tensor(run_max[:], run_max[:], all_mx[:], ALU.max).then_inc(run_max_ready, 1)
                dve.wait_ge(run_max_ready, i + 1)
                nc.vector.tensor_scalar(neg_mx[:], run_max[:], -1.0, None, ALU.mult).then_inc(shift_ready, 1)

            def save_max(i):
                if not upto(i, 0):
                    dve.wait_ge(sums_stored, 16 * i)
                nc.vector.tensor_scalar(sums_out[:, QB:SUMW], run_max[:].to_broadcast([P, SUMW - QB]),
                                        1.0, None, ALU.mult).then_inc(m_saved, 1)

            def mask_probs(i, j):
                dve.wait_ge(exp_ready, HG * i + j + 1)
                four = scores[:, HG * j:HG * (j + 1), :]
                nc.vector.tensor_tensor(four, four, mask_f[:].unsqueeze(1).to_broadcast([P, HG, QB]),
                                        ALU.mult).then_inc(probs_ready, 1)

            def block1(i):
                mask_scores(i)
                running_max(i)
                for c in range(C0):
                    q_low(i + 1, c)
                    if 1 <= c <= HG:
                        mask_probs(i, c - 1)
                save_max(i)

            for c in range(C0):
                q_low(0, c)
            block1(0)
            with dve.Fori(1, NB - 1) as i:
                block1(i)
            mask_scores(NB - 1)
            running_max(NB - 1)

            nc.vector.tensor_scalar(m_eps[:], run_max[:], math.log(SUM_EPS), None, ALU.add).then_inc(m_eps_ready, 1)
            nc.vector.memset(mhalf[:], -0.5).then_inc(mhalf_ready, 1)
            for j in range(HG):
                mask_probs(NB - 1, j)
                dve.wait_ge(k1_hi_ready, j + 1)
                nc.vector.tensor_tensor(k1_lo[:, j, :], A_BANKS[j % 2][:, 0:B * KEYS], f(k1_hi[:, j, :]),
                                        ALU.subtract).then_inc(kv1_done, 1)
            for b in range(B):
                dve.wait_ge(kv1_psum_ready, C1 + b + 1)
                nc.vector.tensor_copy(v1[:, b, :], A_BANKS[(C1 + b) % 2][:]).then_inc(kv1_done, 1)
            save_max(NB - 1)

            def reciprocals0(n, half):
                cols = slice(half * QH, (half + 1) * QH)
                if half == 0:
                    dve.wait_ge(eps_ready, n + 1)
                    nc.vector.tensor_scalar(den[:], sums_in[:, 0:QB], eps_f[:], None, ALU.add).then_inc(den0_ready, 1)
                    dve.wait_ge(den0_ready, n + 1)
                nc.vector.reciprocal(den[:, cols], den[:, cols]).then_inc(rec0_ready, 1)
                if half == 1:
                    dve.wait_ge(rec0_ready, 2 * (n + 1))
                    nc.vector.tensor_copy(r0_hi[:], den[:]).then_inc(r0_hi_ready, 1)
                    dve.wait_ge(r0_hi_ready, n + 1)
                    nc.vector.scalar_tensor_tensor(out=r0_split[:], in0=f(r0_hi[:]), scalar=low_rows[:], in1=den[:],
                                                   op0=ALU.mult, op1=ALU.add).then_inc(r0_ready, 1)

            for c in range(C0):
                dve.wait_ge(wo0_hi_ready, c // 4 + 1)
                nc.vector.tensor_tensor(wo0_lo[:, c, :], w_stage[:, c * D:(c + 1) * D], f(wo0_hi[:, c, :]),
                                        ALU.subtract).then_inc(wo0_ready, 1)
            reciprocals0(0, 0)
            reciprocals0(0, 1)

            def attention0(i, c):
                if c == 0:
                    dve.wait_ge(u_loaded, 16 * (i + 1))
                dve.wait_ge(bc0_ready, C0 * i + c + 1)
                nc.vector.tensor_tensor(u_in[:, c, :], u_in[:, c, :], R_BANKS[c % 2][:],
                                        ALU.mult).then_inc(attn0_ready, 1)

            def x_and_bias(i):
                dve.wait_ge(xn_loaded, 16 * (i + 1))
                nc.vector.tensor_tensor(xn[:], xn[:], bo0_b[:].unsqueeze(1).to_broadcast([P, QT, D]),
                                        ALU.add).then_inc(xb_ready, 1)

            def reciprocals1(i):
                dve.wait_ge(sums1_saved, i + 1)
                nc.vector.tensor_scalar(den[:], den[:], 1e-36, None, ALU.max).then_inc(den1_ready, 1)
                dve.wait_ge(den1_ready, i + 1)
                nc.vector.reciprocal(den[:], den[:]).then_inc(rec1_ready, 1)
                dve.wait_ge(rec1_ready, i + 1)
                nc.vector.tensor_copy(r1_hi[:], den[:]).then_inc(r1_hi_ready, 1)
                dve.wait_ge(r1_hi_ready, i + 1)
                nc.vector.scalar_tensor_tensor(out=r1_split[:], in0=f(r1_hi[:]), scalar=low_rows[:], in1=den[:],
                                               op0=ALU.mult, op1=ALU.add).then_inc(r1_ready, 1)

            def attention1(i):
                dve.wait_ge(u1_saved, C1 * (i + 1))
                for c in range(C1):
                    dve.wait_ge(bc1_ready, C1 * i + c + 1)
                    nc.vector.tensor_tensor(u1[:, c, :], u1[:, c, :], Z_BANKS[c][:],
                                            ALU.mult).then_inc(attn1_ready, 1)

            def rows0(i):
                dve.wait_ge(xb_ready, i + 1)
                for n in range(QT + 2):
                    if n < QT:
                        if n < QT - 1:
                            dve.wait_ge(o0_ready, (QT - 1) * i + n + 1)
                        else:
                            dve.wait_ge(a0_used, C0 * (i + 1))
                        if not upto(i, 0):
                            dve.wait_ge(resid_ready, QT * (i - 1) + n + 1)
                        nc.vector.tensor_tensor(z0[:, n, :], Z_BANKS[n][:], xn[:, n, :], ALU.add).then_inc(z0_ready, 1)
                    if 1 <= n <= QT:
                        dve.wait_ge(z0_ready, QT * i + n)
                        nc.vector.bn_stats(st0[:, n - 1, :], z0[:, n - 1, :]).then_inc(bn0_ready, 1)
                    if n >= 2:
                        dve.wait_ge(bn0_ready, QT * i + n - 1)
                        nc.vector.nop(nofuse=True)
                        nc.vector.bn_aggr(mv0[:, n - 2, :], st0[:, n - 2, :]).then_inc(mv0_ready, 1)

            def norm0(i):
                for n in range(QT):
                    if n % 2 == 0:
                        dve.wait_ge(rstd0_ready, 2 * i + n // 2 + 1)
                    nc.vector.tensor_scalar(z0[:, n, :], z0[:, n, :], mv0[:, n, 0:1], rs0[:, n:n + 1],
                                            ALU.subtract, ALU.mult).then_inc(n0_ready, 1)

            def yt_low(i):
                for c in range(KC):
                    dve.wait_ge(yt_hi_ready, KC * i + c + 1)
                    nc.vector.tensor_tensor(yt_lo[:, c, :], R_BANKS[c][:], f(yt_hi[:, c, :]),
                                            ALU.subtract).then_inc(yt_ready, 1)

            def q1_low(i, chunks):
                for c in chunks:
                    dve.wait_ge(q1_hi_ready, C1 * i + c + 1)
                    nc.vector.scalar_tensor_tensor(out=q1_lo[:, c, :], in0=R_BANKS[c][:], scalar=bq1_sb[:, c:c + 1],
                                                   in1=f(q1_hi[:, c, :]), op0=ALU.add,
                                                   op1=ALU.subtract).then_inc(q1_ready, 1)

            def scores_and_max1(i, c, heads=range(HC1)):
                for g in heads:
                    h = HC1 * c + g
                    dve.wait_ge(logits1_ready, H1 * i + h + 1)
                    nc.vector.tensor_scalar(scores[:, h, :], R_BANKS[g][:], 1.0, -3e38,
                                            ALU.mult, ALU.max, accum_out=mx1[:, h:h + 1]).then_inc(scores1_ready, 1)

            def shift1(i, c):
                dve.wait_ge(amax1_ready, C1 * i + c + 1)
                hs = slice(HC1 * c, HC1 * (c + 1))
                nc.vector.tensor_scalar(sh1[:, hs], amx1[:, hs], -SCALE1, HEADROOM, ALU.mult,
                                        ALU.add).then_inc(shift1_ready, 1)

            def rows1(i):
                dve.wait_ge(resid_ready, QT * (i + 1))
                if not upto(i, 0):
                    dve.wait_ge(out_stored, 16 * i)
                for n in range(QT):
                    row1(i, n)

            def row1(i, n):
                if n < QT - 1:
                    dve.wait_ge(o1_ready, (QT - 1) * i + n + 1)
                else:
                    dve.wait_ge(a1_used, C1 * (i + 1))
                nc.vector.tensor_tensor(z1[:, n, :], Z_BANKS[n][:], resid[:, n, :], ALU.add).then_inc(z1_ready, 1)

            def statistic1(i, n):
                dve.wait_ge(z1_ready, QT * i + n + 1)
                nc.vector.bn_stats(st1[:, n, :], z1[:, n, :]).then_inc(bn1_ready, 1)

            def moments1(i, n):
                dve.wait_ge(bn1_ready, QT * i + n + 1)
                nc.vector.nop(nofuse=True)
                nc.vector.bn_aggr(mv1[:, n, :], st1[:, n, :]).then_inc(mv1_ready, 1)

            def statistics1(i):
                for n in range(QT):
                    statistic1(i, n)
                for n in range(QT):
                    moments1(i, n)

            def center1(i, n):
                dve.wait_ge(rstd1_ready, i + 1)
                nc.vector.scalar_tensor_tensor(out=z1[:, n, :], in0=z1[:, n, :], scalar=mv1[:, n, 0:1],
                                               in1=g1_b[:], op0=ALU.subtract, op1=ALU.mult).then_inc(ng1_ready, 1)

            def scale1(i, n):
                dve.wait_ge(ng1_ready, QT * i + n + 1)
                nc.vector.scalar_tensor_tensor(out=z1[:, n, :], in0=z1[:, n, :], scalar=rs1[:, n:n + 1],
                                               in1=be1_b[:], op0=ALU.mult, op1=ALU.add).then_inc(out_ready, 1)

            def logits_work(i):
                for c in range(C1 - 1):
                    scores_and_max1(i, c)
                    if c < 2:
                        reciprocals0(i + 1, c)
                    shift1(i, c)
                scores_and_max1(i, C1 - 1, range(HC1 - 1))

            def block2(i):
                norm = not upto(i, 1)
                attention0(i, 0)
                scores_and_max1(i - 1, C1 - 1, (HC1 - 1,))
                attention0(i, 1)
                if norm:
                    rows1(i - 2)
                shift1(i - 1, C1 - 1)
                attention0(i, 2)
                if norm:
                    statistics1(i - 2)
                for c in range(3, C0):
                    attention0(i, c)
                    if c == 3:
                        x_and_bias(i)
                    if norm and c >= 4:
                        center1(i - 2, c - 4)
                        if c > 4:
                            scale1(i - 2, c - 5)
                if norm:
                    scale1(i - 2, QT - 1)
                rows0(i)
                norm0(i)
                yt_low(i)
                reciprocals1(i - 1)
                q1_low(i, range(C1 - 1))
                attention1(i - 1)
                q1_low(i, (C1 - 1,))
                logits_work(i)

            for c in range(C0):
                attention0(0, c)
            x_and_bias(0)
            for k in range(KC):
                dve.wait_ge(w1_hi_ready, k + 1)
                last = nc.vector.scalar_tensor_tensor(out=wq1_lo[:, k, :], in0=s_stage[:, k * E1:(k + 1) * E1],
                                                      scalar=g0_col[:, k:k + 1], in1=f(wq1_hi[:, k, :]),
                                                      op0=ALU.mult, op1=ALU.subtract)
            last.then_inc(w1_ready, 1)
            dve.wait_ge(w1_hi_ready, KC + 1)
            dve.wait_ge(u_stored, 16 * NB)
            dve.wait_ge(sums_stored, 16 * NB)
            nc.vector.tensor_tensor(wo1_lo[:].rearrange("p c n -> p (c n)"), s_stage[:, 2048:4096],
                                    f(wo1_hi[:]).rearrange("p c n -> p (c n)"), ALU.subtract).then_inc(w1_ready, 1)
            rows0(0)
            dve.wait_ge(bq1_psum_ready, 1)
            nc.vector.tensor_copy(bq1_sb[:], R_BANKS[3][:, 0:C1]).then_inc(bq1_ready, 1)
            norm0(0)
            yt_low(0)
            q1_low(0, range(C1))
            logits_work(0)
            block2(1)
            with dve.Fori(2, NB) as i:
                block2(i)
            scores_and_max1(NB - 1, C1 - 1, (HC1 - 1,))
            shift1(NB - 1, C1 - 1)
            rows1(NB - 2)
            statistics1(NB - 2)
            reciprocals1(NB - 1)
            center1(NB - 2, 0)
            attention1(NB - 1)
            for n in range(1, QT):
                center1(NB - 2, n)
            for n in range(QT):
                scale1(NB - 2, n)
            dve.wait_ge(resid_ready, QT * NB)
            dve.wait_ge(out_stored, 16 * (NB - 1))
            for n in range(QT + 2):
                if n < QT:
                    row1(NB - 1, n)
                if 1 <= n <= QT:
                    statistic1(NB - 1, n - 1)
                if n >= 2:
                    moments1(NB - 1, n - 2)
            for half in range(2):
                for n in (2 * half, 2 * half + 1):
                    if half == 1:
                        dve.wait_ge(rstd1_ready, NB + 1)
                    center1(NB - 1, n)
                for n in (2 * half, 2 * half + 1):
                    scale1(NB - 1, n)

        @block.gpsimd
        def _(pool):
            def f(ap):
                return ap.bitcast(f32)

            def x_low(i):
                pool.wait_ge(x_hi_ready, i + 1)
                nc.gpsimd.tensor_tensor(x_lo[:], x_raw[:], f(x_hi[:]), ALU.subtract).then_inc(x_ready, 1)

            def all_max(i):
                pool.wait_ge(tile_max_ready, i + 1)
                nc.gpsimd.nop(nofuse=True)
                nc.gpsimd.partition_all_reduce(all_mx[:], tile_mx[:], P, MAX).then_inc(all_max_ready, 1)

            x_low(0)
            x_low(1)
            all_max(0)
            pool.wait_ge(consts_loaded, 16 * 9)
            nc.gpsimd.tensor_tensor(bb1_b[:], bb1_b[:], beta0_b, ALU.add).then_inc(bb1_ready, 1)
            with pool.Fori(1, NB - 1) as i:
                x_low(i + 1)
                all_max(i)
            all_max(NB - 1)

            def a0_low(i, c):
                pool.wait_ge(a0_hi_ready, C0 * i + c + 1)
                nc.gpsimd.tensor_tensor(a_lo[:, c % 2, :], u_in[:, c, :], f(a_hi[:, c % 2, :]),
                                        ALU.subtract).then_inc(a0_ready, 1)

            def a1_low(i, c):
                pool.wait_ge(a1_hi_ready, C1 * i + c + 1)
                nc.gpsimd.tensor_tensor(a_lo[:, c % 2, :], u1[:, c, :], f(a_hi[:, c % 2, :]),
                                        ALU.subtract).then_inc(a1_ready, 1)

            def rstd(tiles, mv, rs, mv_ready, tiles_done, var_ready, rstd_ready, step):
                pool.wait_ge(mv_ready, tiles_done)
                nc.gpsimd.nop(nofuse=True)
                nc.gpsimd.tensor_scalar(rs[:, tiles], mv[:, tiles, 1], LN_EPS, 1.0, ALU.add,
                                        ALU.mult).then_inc(var_ready, 1)
                pool.wait_ge(var_ready, step + 1)
                nc.gpsimd.tensor_tensor(rs[:, tiles], rs[:, tiles], mhalf[:, tiles], ALU.pow).then_inc(rstd_ready, 1)

            def rstd0(i):
                for half in range(2):
                    rstd(slice(2 * half, 2 * half + 2), mv0, rs0, mv0_ready, QT * i + 2 * half + 2,
                         var0_ready, rstd0_ready, 2 * i + half)

            def rstd1(i):
                rstd(slice(0, QT), mv1, rs1, mv1_ready, QT * (i + 1), var1_ready, rstd1_ready, i)

            def residual1(i, c):
                n = c // 2
                if c == 0:
                    pool.wait_ge(n0_ready, QT * (i + 1))
                    if not upto(i, 0):
                        pool.wait_ge(z1_ready, QT * i)
                if c % 2 == 0:
                    nc.gpsimd.tensor_tensor(resid[:, n, :], z0[:, n, :], g0_b[:], ALU.mult).then_inc(rg_ready, 1)
                else:
                    pool.wait_ge(rg_ready, QT * i + n + 1)
                    nc.gpsimd.tensor_tensor(resid[:, n, :], resid[:, n, :], bb1_b[:], ALU.add).then_inc(resid_ready, 1)

            def head_max(i, c):
                pool.wait_ge(scores1_ready, H1 * i + HC1 * (c + 1))
                nc.gpsimd.nop(nofuse=True)
                hs = slice(HC1 * c, HC1 * (c + 1))
                nc.gpsimd.partition_all_reduce(amx1[:, hs], mx1[:, hs], P, MAX).then_inc(amax1_ready, 1)

            def block2(i):
                for c in range(C0):
                    a0_low(i, c)
                    if c == 0:
                        head_max(i - 1, C1 - 1)
                    if c in (1, 2):
                        residual1(i - 1, c - 1)
                    elif c > 3:
                        residual1(i - 1, c - 2)
                    elif c == 3 and not upto(i, 1):
                        rstd1(i - 2)
                residual1(i - 1, C0 - 2)
                residual1(i - 1, C0 - 1)
                rstd0(i)
                a1_low(i - 1, 0)
                a1_low(i - 1, 1)
                a1_low(i - 1, 2)
                head_max(i, 0)
                a1_low(i - 1, 3)
                head_max(i, 1)
                head_max(i, 2)

            for c in range(C0):
                a0_low(0, c)
            pool.wait_ge(mhalf_ready, 1)
            rstd0(0)
            for c in range(C1 - 1):
                head_max(0, c)
            block2(1)
            with pool.Fori(2, NB) as i:
                block2(i)
            head_max(NB - 1, C1 - 1)
            residual1(NB - 1, 0)
            residual1(NB - 1, 1)
            rstd1(NB - 2)
            for c in range(2, C0):
                residual1(NB - 1, c)
            for c in range(C1):
                a1_low(NB - 1, c)
            for half in range(2):
                rstd(slice(2 * half, 2 * half + 2), mv1, rs1, mv1_ready, QT * (NB - 1) + 2 * half + 2,
                     var1_ready, rstd1_ready, NB - 1 + half)


def kernel(x, ctx_1024, mask_BxSxS2_ik1, L0_xattn_Wq, L0_xattn_bq, L0_xattn_Wk, L0_xattn_bk, L0_xattn_Wv,
           L0_xattn_bv, L0_xattn_Wo, L0_xattn_bo, L0_xattn_gamma, L0_xattn_beta, L1_xattn_Wq, L1_xattn_Wk,
           L1_xattn_Wv, L1_xattn_Wo, L1_xattn_bo, L1_xattn_ln_gamma, L1_xattn_ln_beta):
    import concourse.bacc as bacc
    from concourse.bass_utils import run_bass_kernel_spmd

    def blocks(a, last):
        return np.asarray(a).reshape(B, NB, QH, last).transpose(1, 0, 2, 3).reshape(NB, QB, last)

    xb = blocks(x, D)
    mask = blocks(mask_BxSxS2_ik1, KEYS)
    sum_sel = np.zeros((P, HG, 32), np.float32)
    for j in range(HG):
        sum_sel[:, j, j] = sum_sel[:, j, j + HG] = 1
    low_row = np.zeros((P, 1), np.float32)
    for g in range(G):
        low_row[32 * g + HG:32 * g + 2 * HG] = -1

    def head_sel(chunks, width):
        sel = np.zeros((P, chunks, P), np.float32)
        for c in range(chunks):
            for p in range(P):
                h = (c * P + p) // width
                row = 32 * (h % G) + h // G
                sel[row, c, p] = sel[row + HG, c, p] = 1
        return sel.reshape(P, chunks * P)

    def columns(v, chunks):
        return np.asarray(v).reshape(chunks, P).T

    arrays = {
        "x_t": xb.transpose(0, 2, 1), "x_n": xb, "mask_t": mask.transpose(0, 2, 1),
        "ctx_t": np.asarray(ctx_1024).reshape(B * KEYS, D).T,
        "wq0": L0_xattn_Wq, "wk0": L0_xattn_Wk, "wv0": L0_xattn_Wv, "wo0": L0_xattn_Wo,
        "wq1": np.asarray(L1_xattn_Wq).T, "wk1": np.asarray(L1_xattn_Wk).T,
        "wv1": np.asarray(L1_xattn_Wv).T, "wo1": np.asarray(L1_xattn_Wo).T,
        "bq0": columns(L0_xattn_bq, C0), "bk0": columns(L0_xattn_bk, C0), "bv0": L0_xattn_bv,
        "bo0": L0_xattn_bo, "gamma0": L0_xattn_gamma, "beta0": L0_xattn_beta,
        "gcol0": columns(L0_xattn_gamma, KC), "bcol0": columns(L0_xattn_beta, KC),
        "bo1": L1_xattn_bo, "gamma1": L1_xattn_ln_gamma, "beta1": L1_xattn_ln_beta,
        "sum_sel": sum_sel, "low_row": low_row, "head_sel0": head_sel(C0, DK0), "head_sel1": head_sel(C1, DK1),
        "identity": np.eye(P, dtype=np.float32),
    }
    arrays = {k: np.ascontiguousarray(v) for k, v in arrays.items()}
    nc = bacc.Bacc("TRN2", target_bir_lowering=False, num_devices=1, dynamic_dma_scratch_size=2048)
    args = [nc.dram_tensor(k, a.shape, mybir.dt.from_np(a.dtype), kind="ExternalInput").ap()
            for k, a in arrays.items()]
    out = nc.dram_tensor("out", (NB, QB, D), mybir.dt.float32, kind="ExternalOutput").ap()
    cross_attention_program(nc, *args, out)
    r = run_bass_kernel_spmd(nc, [arrays], core_ids=[0])
    return np.asarray(r.results[0]["out"]).reshape(NB, B, QH, D).transpose(1, 0, 2, 3).reshape(B, S, D)
```
